# Optimizing a Trainium2 kernel written in Bass

```python
import numpy as np
import jax
import jax.numpy as jnp

def _softmax(x, axis=-1):
    return jax.nn.softmax(x, axis=axis)
def _gelu(x):
    return jax.nn.gelu(x, approximate=True)
def _silu(x):
    return jax.nn.silu(x)
def _sigmoid(x):
    return jax.nn.sigmoid(x)
def _layernorm(x, axis=-1, eps=1e-5):
    m = jnp.mean(x, axis=axis, keepdims=True)
    v = jnp.var(x, axis=axis, keepdims=True)
    return (x - m) / jnp.sqrt(v + eps)
def _scatter_add(tgt, idx, src, axis=0):
    return tgt.at[idx].add(src)
def _segment_sum(src, seg, n):
    return jax.ops.segment_sum(src, seg, n)

kernel_name = 'mk_adj_preln_d4_adj_64_9318b7'

def setup_inputs(seed: int = 0):
    np.random.seed(seed)
    _w = jnp.asarray
    def _rec_inputs():
        import jax
        import jax.numpy as jnp
        _gk = jax.random.key(seed)
        x = 0.5001 + 0.2887 * jax.random.normal(jax.random.fold_in(_gk, 1), (4096, 64), jnp.float32)
        _w = (1.0 + jnp.arange(4096, dtype=jnp.float32)) ** -0.5
        _w = _w / _w.mean()
        _pij = jnp.clip(0.00390625 * _w[:, None] * _w[None, :], 0.0, 1.0)
        _a = jax.random.uniform(jax.random.fold_in(_gk, 2), (4096, 4096)) < _pij
        _a = jnp.logical_or(_a, jnp.eye(4096, dtype=bool))
        _af = _a.astype(jnp.float32)
        _af = _af * jax.random.uniform(jax.random.fold_in(_gk, 3), (4096, 4096), jnp.float32, 0.05, 1)
        adj = _af
        return x, adj
    x, adj = _rec_inputs()
    def _L0_gnn_setup():
        import jax, jax.numpy as jnp
        import numpy as np
        N = 10000
        DIM = 64
        F_CONST = 1.0
        B_CONST = 0.1
        R_CONST = 0.01
        key = jax.random.key(seed)
        k1, k2 = jax.random.split(key)
        t = jnp.zeros((1,), dtype=jnp.float32)
        x = jax.random.uniform(k1, (N, DIM), dtype=jnp.float32)
        A = jax.random.uniform(k2, (N, N), dtype=jnp.float32)
        return {'t': t, 'x': x, 'A': A}
    _L0_gnn_all = _L0_gnn_setup()
    _L0_gnn_in = {k: v for k, v in _L0_gnn_all.items() if k in ('t', )}
    del _L0_gnn_all

    def _L1_gnn_setup():
        import jax, jax.numpy as jnp
        import numpy as np
        HOP = 2
        N = 16384
        HIDDEN = 64
        key = jax.random.key(seed)
        k1, k2, k3 = jax.random.split(key, 3)
        user_embs = jax.random.normal(k1, (N, HIDDEN), dtype=jnp.float32)
        adj = jax.random.uniform(k2, (N, N), dtype=jnp.float32)
        limit = float(np.sqrt(6.0 / (2 * HIDDEN + HIDDEN)))
        W = jax.random.uniform(k3, (HOP, 2 * HIDDEN, HIDDEN), dtype=jnp.float32, minval=-limit, maxval=limit)
        return {'user_embs': user_embs, 'adj': adj, 'W': W}
    _L1_gnn_all = _L1_gnn_setup()
    _L1_gnn_in = {k: v for k, v in _L1_gnn_all.items() if k in ('W', )}
    del _L1_gnn_all

    def _L2_gnn_setup():
        import jax, jax.numpy as jnp
        import numpy as np
        N, D_IN, D_OUT = (8192, 64, 64)
        MAX_NEIGH = 100
        DECAY = 0.5
        key = jax.random.key(seed)
        k1, k2, k3, k4 = jax.random.split(key, 4)
        stdv = 1.0 / np.sqrt(D_OUT)
        inputs = {'input': jax.random.normal(k1, (N, D_IN), dtype=jnp.float32), 'adj': jax.random.randint(k2, (N, N), 0, 2).astype(jnp.float32), 'weight': jax.random.uniform(k3, (D_IN, D_OUT), minval=-stdv, maxval=stdv, dtype=jnp.float32), 'bias': jax.random.uniform(k4, (D_OUT,), minval=-stdv, maxval=stdv, dtype=jnp.float32)}
        return inputs
    _L2_gnn_all = _L2_gnn_setup()
    _L2_gnn_in = {k: v for k, v in _L2_gnn_all.items() if k in ('weight', 'bias', )}
    del _L2_gnn_all

    def _L3_gnn_setup():
        import jax, jax.numpy as jnp
        import numpy as np
        N, D, H = (16384, 64, 256)
        GAIN = 0.2
        key = jax.random.key(seed)
        ks = jax.random.split(key, 6)
        X = jax.random.normal(ks[0], (N, D), dtype=jnp.float32)
        t = jax.random.uniform(ks[1], (1,), dtype=jnp.float32)
        Wt = jax.random.uniform(ks[2], (N, N), dtype=jnp.float32)
        B = GAIN * jnp.eye(D, dtype=jnp.float32) + 0.01 * jax.random.normal(ks[3], (D, D), dtype=jnp.float32)
        W1 = jax.random.normal(ks[4], (D + 1, H), dtype=jnp.float32) * (1.0 / np.sqrt(D + 1))
        b1 = jnp.zeros((H,), dtype=jnp.float32)
        W2 = jax.random.normal(ks[5], (H, D), dtype=jnp.float32) * (1.0 / np.sqrt(H))
        b2 = jnp.zeros((D,), dtype=jnp.float32)
        return {'X': X, 't': t, 'Wt': Wt, 'B': B, 'W1': W1, 'b1': b1, 'W2': W2, 'b2': b2}
    _L3_gnn_all = _L3_gnn_setup()
    _L3_gnn_in = {k: v for k, v in _L3_gnn_all.items() if k in ('t', 'B', 'W1', 'b1', 'W2', 'b2', )}
    del _L3_gnn_all

    return {
        "x": x,
        "adj": adj,
        "L0_gnn_t": _L0_gnn_in["t"],
        "L1_gnn_W": _L1_gnn_in["W"],
        "L2_gnn_weight": _L2_gnn_in["weight"],
        "L2_gnn_bias": _L2_gnn_in["bias"],
        "L3_gnn_t": _L3_gnn_in["t"],
        "L3_gnn_B": _L3_gnn_in["B"],
        "L3_gnn_W1": _L3_gnn_in["W1"],
        "L3_gnn_b1": _L3_gnn_in["b1"],
        "L3_gnn_W2": _L3_gnn_in["W2"],
        "L3_gnn_b2": _L3_gnn_in["b2"],
    }

def reference(x, adj, L0_gnn_t, L1_gnn_W, L2_gnn_weight, L2_gnn_bias, L3_gnn_t, L3_gnn_B, L3_gnn_W1, L3_gnn_b1, L3_gnn_W2, L3_gnn_b2):
    import jax
    import jax.numpy as jnp
    def _L0_gnn_ref(t, x, A):
        import jax, jax.numpy as jnp
        import numpy as np
        N = 10000
        DIM = 64
        F_CONST = 1.0
        B_CONST = 0.1
        R_CONST = 0.01
        Ax = A @ x
        outer = R_CONST * jnp.sum(x * Ax, axis=1, keepdims=True)
        return F_CONST - B_CONST * x - outer

    def _L1_gnn_ref(user_embs, adj, W):
        import jax, jax.numpy as jnp
        import numpy as np
        HOP = 2
        N = 16384
        HIDDEN = 64
        x = user_embs
        for k in range(HOP):
            agg = adj @ x
            x = jnp.tanh(jnp.concatenate([agg, x], axis=1) @ W[k])
        return x

    def _L2_gnn_ref(input, adj, weight, bias):
        import jax, jax.numpy as jnp
        import numpy as np
        N, D_IN, D_OUT = (8192, 64, 64)
        MAX_NEIGH = 100
        DECAY = 0.5
        support = input @ weight
        mask = (adj != 0).astype(support.dtype)
        rank = jnp.cumsum(mask, axis=1)
        deg = rank[:, -1:]
        k = jnp.minimum(deg, float(MAX_NEIGH))
        pos = rank - (deg - k)
        w = mask * jnp.where(pos > 0, DECAY ** (k - pos), 0.0)
        out = w @ support + bias
        return out

    def _L3_gnn_ref(X, t, Wt, B, W1, b1, W2, b2):
        import jax, jax.numpy as jnp
        import numpy as np
        N, D, H = (16384, 64, 256)
        GAIN = 0.2
        n = X.shape[0]
        tcol = jnp.broadcast_to(t.reshape(1, 1), (n, 1))
        h = jnp.tanh(jnp.concatenate([X, tcol], axis=1) @ W1 + b1)
        u_intra = h @ W2 + b2
        XB = X @ B.T
        u_comm = Wt @ XB - jnp.sum(Wt, axis=1, keepdims=True) * XB
        return u_intra + u_comm

    h = jnp.maximum(_layernorm(x, axis=-1), 0.0)
    x = x + _L0_gnn_ref(L0_gnn_t, h, adj)
    h = jnp.maximum(_layernorm(x, axis=-1), 0.0)
    x = x + _L1_gnn_ref(h, adj, L1_gnn_W)
    h = jnp.maximum(_layernorm(x, axis=-1), 0.0)
    x = x + _L2_gnn_ref(h, adj, L2_gnn_weight, L2_gnn_bias)
    h = jnp.maximum(_layernorm(x, axis=-1), 0.0)
    x = x + _L3_gnn_ref(h, L3_gnn_t, adj, L3_gnn_B, L3_gnn_W1, L3_gnn_b1, L3_gnn_W2, L3_gnn_b2)
    return x


_drawn_inputs = setup_inputs


def setup_inputs(seed=0):
    import zlib

    import numpy as np

    out = dict(_drawn_inputs(seed))
    spreads = {'L3_gnn_b1': (0.0, 0.1), 'L3_gnn_b2': (0.0, 0.1)}
    factors = {}
    for name, (base, spread) in spreads.items():
        noise = np.random.default_rng([zlib.crc32(name.encode()), seed]).standard_normal(out[name].shape)
        drawn = base * np.exp(spread * noise) if base else spread * noise
        out[name] = jnp.asarray(drawn.astype(out[name].dtype))
    for name, factor in factors.items():
        out[name] = (out[name] * factor).astype(out[name].dtype)
    return out
```

```python
from contextlib import ExitStack

import numpy as np

import concourse.bass as bass
from concourse import mybir

ALU = mybir.AluOpType
ACT = mybir.ActivationFunctionType
AX_X = mybir.AxisListType.X
F32 = mybir.dt.float32
F16 = mybir.dt.float16
BF16 = mybir.dt.bfloat16
U16 = mybir.dt.uint16

P = 128
N = 4096
D = 64
NT = N // P
W = 512
NC = N // W
TQ = 4
NQ = NT // TQ
BLK = TQ * W
EPS = 1e-5
PRO_GROUPS = 4

L0, L1A, L1B, L2, L3 = range(5)
SPLIT_SWEEPS = (L0, L1A, L1B, L3)
CACHED = (0, 4)
RINGED = (1, 2, 3, 5, 6, 7)
NR = len(RINGED)

SCALE = 4096.0
UNSCALE = 1.0 / (SCALE * SCALE)
NEIGH = 100
BIT = 128.0
L2_UNSCALE = 2.0 ** (127 - NEIGH) / SCALE
XW = 2 * D + 2

COLS = {}
_at = 0
for _name, _n in (("wagg0", D), ("wx0", D), ("wagg1", D), ("wx1", D), ("l2w", D), ("bT", D), ("w1", 256),
                  ("w2", 2 * D), ("w1t", 2), ("b1", 2), ("t", 1), ("bias", D), ("b2", D),
                  ("ident", P), ("joinA", D + 1), ("joinB", D + 1)):
    COLS[_name] = (_at, _at + _n)
    _at += _n
NCOLS = _at
LN_STEPS = 5
EPI_LINKS = {L0: 4 + LN_STEPS + 2, L1A: 1, L1B: LN_STEPS + 1, L2: 1 + LN_STEPS + 1, L3: 3}


def loaded(p):
    if p == L0:
        return list(range(NQ))
    return list(reversed(RINGED)) if p == L2 else list(RINGED)


def slot_use(p, s, q):
    first = q < 4 if p != L2 else q >= 4
    return 2 * s + (0 if first else 1)


def split_no(p, c, q):
    if p == L0:
        return NQ * c + q
    before = {L1A: 0, L1B: 1, L3: 2}[p]
    return NQ * NC + NR * NC * before + NR * c + RINGED.index(q)


def ring_no(p, c, q):
    return NR * (NC * SPLIT_SWEEPS.index(p) + c) + RINGED.index(q)


def nat_no(p, c, i=0):
    return {L0: c, L1A: 8 + c, L1B: 16 + 2 * c + i, L2: 32 + 3 * c + i, L3: 56 + c}[p]


def tr_no(p, c, i=0):
    return {L1A: c, L1B: 8 + 2 * c + i, L2: 24 + 3 * c + i}[p]


def row_no(p, c):
    return {L0: c, L1B: 8 + c, L2: 16 + c, L3: 24 + c}[p]


def ready_no(p, c):
    return {L0: 0, L2: NC, L3: 2 * NC}[p] + c


def norm_no(p, c):
    return PRO_GROUPS + {L0: 0, L1B: NC, L2: 2 * NC}[p] + c


def link_base(p, c):
    return PROLOGUE_LINKS + sum(NC * EPI_LINKS[k] for k in range(p)) + EPI_LINKS[p] * c


PROLOGUE_LINKS = PRO_GROUPS * (LN_STEPS + 2)


def sweep_steps(eng, step, finish):
    for p in range(5):
        step(p, 0, 0, (p - 1, NC - 1, 1) if p else None)
        start = 1
        if p == L0:
            step(p, 1, 1, (p, 0, 0))
            step(p, 2, 0, (p, 1, 1))
            start = 3
        with eng.Fori(start, NC - 1, 2) as c:
            step(p, c, 1, (p, c - 1, 0))
            step(p, c + 1, 0, (p, c, 1))
        step(p, NC - 1, 1, (p, NC - 2, 0))
    finish((L3, NC - 1, 1))


def gnn_kernel(nc, x_in, adj_in, wts_in, tri_in, out):
    x1_d = nc.dram_tensor("x1_rows", (P, NT * D), F32, kind="Internal").ap()
    x2_d = nc.dram_tensor("x2_rows", (P, NT * D), F32, kind="Internal").ap()
    x3_d = nc.dram_tensor("x3_rows", (P, NT * D), F32, kind="Internal").ap()
    rows_from = {L0: x_in, L1B: x1_d, L2: x2_d, L3: x3_d}
    rows_to = {L0: x1_d, L1B: x2_d, L2: x3_d, L3: out}

    with ExitStack() as ctx:
        def sb(name, shape, dt):
            return ctx.enter_context(nc.sbuf_tensor(name, shape, dt))

        def psum(name, shape, dt):
            return ctx.enter_context(nc.psum_tensor(name, shape, dt))

        def sem(name):
            return ctx.enter_context(nc.semaphore(name))

        cache = sb("cache", [P, NC * 2 * 2 * BLK], F16)
        ring = sb("ring", [P, 2, 2 * BLK], F16)
        land = sb("land", [P, 4, BLK], F32)
        X = [sb(f"X{i}", [P, NT * XW], F16) for i in range(2)]
        wts = sb("wts", [P, NCOLS], F32)
        ident16 = sb("ident16", [P, P], F16)
        ones16 = sb("ones16", [P, D + 2], F16)
        triA = sb("triA", [P, P], BF16)
        triB = sb("triB", [P, P], BF16)
        accS = sb("accS", [P, W], F32)
        accBS = sb("accBS", [P, W], F32)
        natS = sb("natS", [P, 4 * (D + 1)], F32)
        xin = sb("xin", [P, 4 * D], F32)
        zS = sb("zS", [P, 4 * D], F32)
        tS = sb("tS", [P, 4 * D], F32)
        hS = sb("hS", [P, 4 * D], F32)
        rowsum = sb("rowsum", [P, NT], F32)
        st = sb("st", [P, 16], F32)
        var = sb("var", [P, 8], F32)
        rstd = sb("rstd", [P, 8], F32)
        power = sb("power", [P, 8], F32)
        hbias = sb("hbias", [P, 2], F32)
        uS = ring[:, 0, :].bitcast(BF16)
        wS = ring[:, 1, :]
        hidS = land[:, 0, :]
        x_all = cache[:, 15 * 2 * BLK:16 * 2 * BLK].bitcast(F32)
        pro = cache[:, 14 * 2 * BLK:15 * 2 * BLK].bitcast(F32)
        tri_f = cache[:, 13 * 2 * BLK:14 * 2 * BLK].bitcast(F32)

        accA = psum("accA", [P, 2, W], F32)
        spare = psum("spare", [P, 4, W], F32)
        nat = psum("nat", [P, W], F32)
        tr = psum("tr", [P, W], F32)

        landed = [sem(f"landed{i}") for i in range(4)]
        wts_in_s, tri_in_s, x_in_s = sem("wts_in"), sem("tri_in"), sem("x_in")
        hi_ready = sem("hi_ready")
        split_ready = sem("split_ready")
        ring_done = sem("ring_done")
        acc_evac, accb_evac = sem("acc_evac"), sem("accb_evac")
        nat_done, nat_evac, nat_used = sem("nat_done"), sem("nat_evac"), sem("nat_used")
        tr_done, tr_evac = sem("tr_done"), sem("tr_evac")
        h_ready = sem("h_ready")
        x_ready = sem("x_ready")
        link = sem("link")
        const_ready = sem("const_ready")
        rows_in, rows_out = sem("rows_in"), sem("rows_out")
        rows_used, rows_ready = sem("rows_used"), sem("rows_ready")
        var_ready, rstd_ready = sem("var_ready"), sem("rstd_ready")
        power_ready = sem("power_ready")
        u_ready = sem("u_ready")
        tri_done = sem("tri_done")
        w_ready = sem("w_ready")
        w_used = sem("w_used")

        def wt(name, rows=P, lo=0, hi=None):
            a, b = COLS[name]
            return wts[0:rows, a + lo:(b if hi is None else a + hi)]

        def chunk_tiles(x, c, lo, n):
            v = x[:, bass.ds(c * (4 * XW), 4 * XW)].rearrange("p (t w) -> p t w", w=XW)
            return v[:, :, lo:lo + n]

        def tile(x, t, lo, n):
            return x[:, t * XW + lo:t * XW + lo + n]

        def cached(c, q, part, k=0, n=TQ):
            return cache[:, bass.ds(c * (4 * BLK) + ((q // 4) * 2 + part) * BLK + k * W, n * W)]

        def ringed(r, part, k=0, n=TQ):
            return ring[:, r % 2, part * BLK + k * W:part * BLK + (k + n) * W]

        def rows4(t):
            return t[:, 0:4 * D].rearrange("p (t d) -> p t d", d=D)

        def spread(col):
            return col.rearrange("p (t o) -> p t o", o=1).to_broadcast([P, col.shape[1], D])

        def over_tiles(name):
            return wt(name).rearrange("p (o d) -> p o d", o=1).to_broadcast([P, 4, D])

        block = ctx.enter_context(nc.Block())

        @block.sync
        def _(sp):
            sp.dma_start(x_all, x_in).then_inc(x_in_s, 16)
            sp.dma_start(wts[:, :], wts_in).then_inc(wts_in_s, 16)
            sp.dma_start(tri_f[:, 0:2 * P], tri_in).then_inc(tri_in_s, 16)

            def step(p, c, par, before):
                qs = loaded(p)
                for i, q in enumerate(qs):
                    if p == L0:
                        if i >= 4:
                            sp.wait_ge(split_ready, split_no(p, c, q - 4) + 1)
                        elif not (isinstance(c, int) and c == 0):
                            sp.wait_ge(split_ready, split_no(p, c - 1, q + 4) + 1)
                    else:
                        if i >= 3:
                            pp, pc, pq = p, c, qs[i - 3]
                        elif isinstance(c, int) and c == 0:
                            pp, pc = p - 1, NC - 1
                            pq = [b for b in loaded(pp) if b % 4 == q % 4][-1]
                        else:
                            pp, pc, pq = p, c - 1, qs[i + 3]
                        if pp == L2:
                            sp.wait_ge(u_ready, NT * pc + NT - TQ * pq)
                        else:
                            sp.wait_ge(split_ready, split_no(pp, pc, pq) + 1)
                    sp.dma_start(land[:, q % 4, :], adj_in[bass.ds(c * (NQ * P) + q * P, P), :])\
                        .then_inc(landed[q % 4], 16)

            sweep_steps(sp, step, lambda before: None)

        @block.gpsimd
        def _(pool):
            def inverse_root(number, ntile):
                pool.wait_ge(var_ready, number + 1)
                nc.gpsimd.tensor_tensor(rstd[:, 0:ntile], var[:, 0:ntile], power[:, 0:ntile], ALU.pow)\
                    .then_inc(rstd_ready, 1)

            nc.gpsimd.memset(power[:, :], -0.5).then_inc(power_ready, 1)
            pool.wait_ge(power_ready, 1)
            for g in range(PRO_GROUPS):
                inverse_root(g, 8)
            with pool.Fori(0, 3 * NC) as c:
                inverse_root(PRO_GROUPS + c, 4)

        @block.scalar
        def _(act):
            def xin_read(p, c):
                if p == L0:
                    act.wait_ge(rows_used, c + 1)
                else:
                    act.wait_ge(nat_used, nat_no(p, c, 0) + 1)

            def epilogue(at, e):
                p, c, par = e
                if at == 0 and p in rows_from:
                    if not (isinstance(c, int) and c == 0):
                        xin_read(p, c - 1)
                    elif p != L0:
                        xin_read({L1B: L0, L2: L1B, L3: L2}[p], NC - 1)
                    act.dma_start(xin[:, :], rows_from[p][:, bass.ds(c * (4 * D), 4 * D)]).then_inc(rows_in, 16)
                if at == 1:
                    if p == L2:
                        act.wait_ge(w_used, 16 * (c + 1))
                    else:
                        act.wait_ge(ring_done, ring_no(p, c, NQ - 1) + 1)
                    if not (isinstance(c, int) and c == 0 and p == L0):
                        act.wait_ge(nat_done, nat_no(p, c, 0))
                    nc.scalar.activation(accS[:, :], accA[:, par, :], ACT.Copy,
                                         scale=L2_UNSCALE if p == L2 else UNSCALE).then_inc(acc_evac, 1)
                    if p == L0:
                        nc.scalar.activation(accBS[0:D + 2, :], spare[0:D + 2, par, :], ACT.Copy, scale=UNSCALE)\
                            .then_inc(accb_evac, 1)
                    if p in (L1A, L1B):
                        act.wait_ge(tr_done, tr_no(p, c, 0) + 1)
                        nc.scalar.activation(accBS[:, :], tr[:, 0:W // 2].bitcast(F16), ACT.Copy, scale=1.0 / SCALE)\
                            .then_inc(tr_evac, 1)
                if at == 3:
                    n = nat_no(p, c, 0)
                    act.wait_ge(nat_done, n + 1)
                    if not (isinstance(n, int) and n == 0):
                        act.wait_ge(nat_used, n)
                    width = 4 * (D + 1) if p == L0 else 4 * D
                    nc.scalar.activation(natS[:, 0:width], nat[:, 0:width],
                                         ACT.Tanh if p in (L1A, L1B) else ACT.Copy).then_inc(nat_evac, 1)
                if at == 5 and p in (L1B, L2):
                    i = 1 if p == L1B else 0
                    act.wait_ge(tr_done, tr_no(p, c, i) + 1)
                    nc.scalar.activation(accBS[0:D, :], tr[0:D, :], ACT.Copy).then_inc(tr_evac, 1)
                if at == 6 and p in (L1B, L2):
                    n = nat_no(p, c, 1)
                    act.wait_ge(nat_done, n + 1)
                    act.wait_ge(nat_used, n)
                    nc.scalar.activation(natS[:, 0:4 * D], nat[:, 0:4 * D], ACT.Copy, scale=SCALE)\
                        .then_inc(nat_evac, 1)
                if p == L2 and at in (6, 7):
                    h = at - 6
                    act.wait_ge(tr_done, tr_no(p, c, 1 + h) + 1)
                    nc.scalar.activation(hidS[:, h * W:(h + 1) * W], tr[:, :], ACT.Tanh, bias=hbias[:, h:h + 1])\
                        .then_inc(tr_evac, 1)
                if p == L2 and at == 7:
                    n = nat_no(p, c, 2)
                    act.wait_ge(nat_done, n + 1)
                    act.wait_ge(nat_used, n)
                    nc.scalar.activation(natS[:, 0:4 * D], nat[:, 0:4 * D], ACT.Copy).then_inc(nat_evac, 1)

                if at == 7 and p in rows_to:
                    if p == L1B:
                        act.wait_ge(nat_used, nat_no(p, c, 0) + 1)
                    else:
                        act.wait_ge(rows_ready, ready_no(p, c) + 1)
                    act.dma_start(rows_to[p][:, bass.ds(c * (4 * D), 4 * D)], zS[:, :]).then_inc(rows_out, 16)

            def main(p, c, par, b):
                if p == L2:
                    for pair in (2 * b, 2 * b + 1):
                        act.wait_ge(tri_done, 16 * c + pair + 1)
                        if pair >= 4 or not (isinstance(c, int) and c == 0):
                            act.wait_ge(w_used, 16 * c + pair - 3)
                        k = pair % 2
                        nc.scalar.activation(wS[:, (pair % 4) * 2 * W:(pair % 4 + 1) * 2 * W].bitcast(U16),
                                             spare[:, 2 * k:2 * k + 2, :].rearrange("p a b -> p (a b)"), ACT.Relu)\
                            .then_inc(w_ready, 1)
                    return
                q = b
                if q not in loaded(p):
                    return
                s = NC * p + c
                act.wait_ge(landed[q % 4], (slot_use(p, s, q) + 1) * 16)
                if p == L0 and q in CACHED:
                    hi = cached(c, q, 0)
                else:
                    n = ring_no(p, c, q)
                    if not (isinstance(n, int) and n < 2):
                        act.wait_ge(ring_done, n - 1)
                    if p == L3 and isinstance(c, int) and c == 0 and q == RINGED[1]:
                        act.wait_ge(w_used, 16 * NC)
                    hi = ringed(RINGED.index(q), 0)
                nc.scalar.activation(hi, land[:, q % 4, :], ACT.Copy, scale=SCALE).then_inc(hi_ready, 1)

            def step(p, c, par, before):
                early = p == L2 and isinstance(c, int) and c == 0
                if early:
                    for b in range(NQ):
                        epilogue(b, before)
                for b in range(NQ):
                    main(p, c, par, b)
                    if before and not early:
                        epilogue(b, before)

            def finish(before):
                for b in range(NQ):
                    epilogue(b, before)
                act.wait_ge(rows_out, 16 * 4 * NC)

            act.wait_ge(const_ready, 1)
            sweep_steps(act, step, finish)

        @block.vector
        def _(dve):
            class Links:
                def __init__(self, base):
                    self.base, self.n = base, 0

                def wait(self):
                    dve.wait_ge(link, self.base + self.n)

                def __call__(self, ins):
                    ins.then_inc(link, 1)
                    self.n += 1
                    self.wait()

            def layernorm(L, z, t, s0, ntile, number):
                s1, s2 = st[:, 0:ntile], st[:, 8:8 + ntile]
                zv = z.rearrange("p (t d) -> p t d", d=D)
                tv = t.rearrange("p (t d) -> p t d", d=D)
                qv = s0.rearrange("p (t d) -> p t d", d=D)
                L(nc.vector.tensor_reduce(s1, zv, AX_X, ALU.add))
                L(nc.vector.scalar_tensor_tensor(out=tv, in0=spread(s1), scalar=-1.0 / D, in1=zv,
                                                 op0=ALU.mult, op1=ALU.add))
                L(nc.vector.tensor_tensor(qv, tv, tv, ALU.mult))
                L(nc.vector.tensor_reduce(s2, qv, AX_X, ALU.add))
                nc.vector.tensor_scalar(var[:, 0:ntile], s2, D * EPS, None, ALU.add).then_inc(var_ready, 1)
                dve.wait_ge(rstd_ready, number + 1)
                L(nc.vector.tensor_tensor(tv, tv, spread(rstd[:, 0:ntile]), ALU.mult))

            def epilogue(at, e):
                p, c, par = e
                nv = rows4(natS)
                nxt = X[(p + 1) % 2]
                hi, lo = (chunk_tiles(nxt, c, 2, D), chunk_tiles(nxt, c, 2 + D, D)) if p != L3 else (None, None)
                here = X[p % 2]
                mine = (chunk_tiles(here, c, 2, D), chunk_tiles(here, c, 2 + D, D))
                if at == 4:
                    L = Links(link_base(p, c))
                    k = None if p == L1A else row_no(p, c)
                    n = nat_no(p, c, 0)
                    dve.wait_ge(nat_evac, n + 1)
                    if p != L1A:
                        dve.wait_ge(rows_in, (k + 1) * 16)
                        if not (isinstance(k, int) and k == 0):
                            dve.wait_ge(rows_out, k * 16)
                    if p == L0:
                        n5 = natS[:, 0:4 * (D + 1)].rearrange("p (t d) -> p t d", d=D + 1)
                        agg = n5[:, :, 0:D]
                        L(nc.vector.tensor_tensor(rows4(hS), mine[0], mine[1], ALU.add))
                        L(nc.vector.tensor_tensor(rows4(tS), rows4(hS), agg, ALU.mult))
                        L(nc.vector.tensor_reduce(st[:, 0:4], rows4(tS), AX_X, ALU.add))
                        nc.vector.tensor_copy(rowsum[:, bass.ds(c * 4, 4)].rearrange("p (t o) -> p t o", o=1),
                                              n5[:, :, D:D + 1]).then_inc(nat_used, 1)
                        L(nc.vector.tensor_scalar(st[:, 8:12], st[:, 0:4], -0.01 / SCALE, 1.0, ALU.mult, ALU.add))
                        nc.vector.scalar_tensor_tensor(out=tS[:, :], in0=hS[:, :], scalar=-0.1 / SCALE,
                                                       in1=xin[:, :], op0=ALU.mult, op1=ALU.add).then_inc(rows_used, 1)
                        dve.wait_ge(rows_used, k + 1)
                        nc.vector.tensor_tensor(rows4(zS), rows4(tS), spread(st[:, 8:12]), ALU.add)\
                            .then_inc(rows_ready, 1)
                        dve.wait_ge(rows_ready, ready_no(p, c) + 1)
                        layernorm(L, zS[:, :], tS[:, :], hS[:, :], 4, norm_no(p, c))
                        L(nc.vector.tensor_scalar(hS[:, :], tS[:, :], 0.0, 8.0 * SCALE, ALU.max, ALU.mult))
                        L(nc.vector.tensor_copy(hi, rows4(hS)))
                        nc.vector.tensor_tensor(lo, rows4(hS), hi, ALU.subtract).then_inc(x_ready, 1)
                    elif p == L1A:
                        nc.vector.tensor_scalar(hS[:, :], natS[:, 0:4 * D], SCALE, None, ALU.mult).then_inc(nat_used, 1)
                        dve.wait_ge(nat_used, n + 1)
                        L(nc.vector.tensor_copy(hi, rows4(hS)))
                        nc.vector.tensor_tensor(lo, rows4(hS), hi, ALU.subtract).then_inc(x_ready, 1)
                    elif p == L1B:
                        nc.vector.tensor_tensor(zS[:, :], xin[:, :], natS[:, 0:4 * D], ALU.add).then_inc(nat_used, 1)
                        dve.wait_ge(nat_used, n + 1)
                        layernorm(L, zS[:, :], tS[:, :], hS[:, :], 4, norm_no(p, c))
                        nc.vector.tensor_scalar(hS[:, :], tS[:, :], 0.0, 8.0, ALU.max, ALU.mult).then_inc(h_ready, 1)
                    elif p == L2:
                        nc.vector.tensor_tensor(tS[:, :], xin[:, :], natS[:, 0:4 * D], ALU.add).then_inc(nat_used, 1)
                        dve.wait_ge(nat_used, n + 1)
                        L(nc.vector.tensor_tensor(rows4(zS), rows4(tS), over_tiles("bias"), ALU.add))
                        layernorm(L, zS[:, :], tS[:, :], hS[:, :], 4, norm_no(p, c))
                        nc.vector.tensor_scalar(hS[:, :], tS[:, :], 0.0, 8.0, ALU.max, ALU.mult).then_inc(h_ready, 1)
                    else:
                        L(nc.vector.tensor_tensor(rows4(hS), mine[0], mine[1], ALU.add))
                        L(nc.vector.tensor_scalar(st[:, 0:4], rowsum[:, bass.ds(c * 4, 4)], -1.0 / SCALE, None, ALU.mult))
                        L(nc.vector.tensor_tensor(rows4(tS), rows4(hS), spread(st[:, 0:4]), ALU.mult))
                        nc.vector.tensor_tensor(hS[:, :], xin[:, :], natS[:, 0:4 * D], ALU.add).then_inc(nat_used, 1)
                        dve.wait_ge(nat_used, n + 1)
                        nc.vector.tensor_tensor(zS[:, :], hS[:, :], tS[:, :], ALU.add).then_inc(rows_ready, 1)
                if at == 7 and p in (L1B, L2):
                    L = Links(link_base(p, c) + EPI_LINKS[p] - 1)
                    dve.wait_ge(nat_evac, nat_no(p, c, 1) + 1)
                    L(nc.vector.tensor_copy(hi, rows4(natS)))
                    nc.vector.tensor_tensor(lo, rows4(natS), hi, ALU.subtract).then_inc(nat_used, 1)
                if at == 7 and p == L2:
                    dve.wait_ge(nat_evac, nat_no(p, c, 2) + 1)
                    nc.vector.tensor_tensor(tS[:, :], zS[:, :], natS[:, 0:4 * D], ALU.add).then_inc(nat_used, 1)
                    dve.wait_ge(nat_used, nat_no(p, c, 2) + 1)
                    nc.vector.tensor_tensor(rows4(zS), rows4(tS), over_tiles("b2"), ALU.add).then_inc(rows_ready, 1)

            def main(p, c, par, b):
                if p == L2:
                    q = NQ - 1 - b
                    if q not in CACHED:
                        dve.wait_ge(landed[q % 4], (slot_use(p, NC * p + c, q) + 1) * 16)
                    for i in range(TQ):
                        k = TQ - 1 - i
                        t = TQ * b + i
                        src = cached(c, q, 0, k, 1) if q in CACHED else land[:, q % 4, k * W:(k + 1) * W]
                        u = uS[:, (t % 8) * W:(t % 8 + 1) * W]
                        if t >= 8 or not (isinstance(c, int) and c == 0):
                            dve.wait_ge(tri_done, 16 * c + (t - 7) // 2 + 1)
                        if t == 0:
                            nc.vector.tensor_scalar(u, src, 0.0, None, ALU.not_equal).then_inc(u_ready, 1)
                        else:
                            dve.wait_ge(u_ready, NT * c + t)
                            prev = uS[:, ((t - 1) % 8) * W:((t - 1) % 8 + 1) * W]
                            nc.vector.scalar_tensor_tensor(out=u, in0=src, scalar=0.0, in1=prev,
                                                           op0=ALU.not_equal, op1=ALU.add).then_inc(u_ready, 1)
                    return
                q = b
                if q not in loaded(p):
                    return
                n = split_no(p, c, q)
                dve.wait_ge(hi_ready, n + 1)
                if p == L0 and q in CACHED:
                    hi, lo = cached(c, q, 0), cached(c, q, 1)
                else:
                    hi, lo = ringed(RINGED.index(q), 0), ringed(RINGED.index(q), 1)
                nc.vector.scalar_tensor_tensor(out=lo, in0=land[:, q % 4, :], scalar=SCALE, in1=hi,
                                               op0=ALU.mult, op1=ALU.subtract).then_inc(split_ready, 1)

            def step(p, c, par, before):
                early = p == L2 and isinstance(c, int) and c == 0
                first = p == L0 and isinstance(c, int) and c == 0
                if early:
                    for b in range(NQ):
                        epilogue(b, before)
                for b in range(NQ):
                    if first and b % 2 == 0:
                        prologue_group(b // 2)
                    main(p, c, par, b)
                    if before and not early:
                        epilogue(b, before)

            def finish(before):
                for b in range(NQ):
                    epilogue(b, before)

            def prologue_group(g):
                L = Links(g * (LN_STEPS + 2))
                n = 8 * D
                z, t, s0 = x_all[:, g * n:(g + 1) * n], pro[:, 0:n], pro[:, n:2 * n]
                layernorm(L, z, t, s0, 8, g)
                L(nc.vector.tensor_scalar(s0, t, 0.0, 8.0 * SCALE, ALU.max, ALU.mult))
                v = X[0][:, g * 8 * XW:(g + 1) * 8 * XW].rearrange("p (t w) -> p t w", w=XW)
                sv = s0.rearrange("p (t d) -> p t d", d=D)
                L(nc.vector.tensor_copy(v[:, :, 2:2 + D], sv))
                nc.vector.tensor_tensor(v[:, :, 2 + D:2 + 2 * D], sv, v[:, :, 2:2 + D], ALU.subtract)\
                    .then_inc(x_ready, 1)

            dve.wait_ge(wts_in_s, 16)
            dve.wait_ge(tri_in_s, 16)
            dve.wait_ge(x_in_s, 16)
            nc.vector.tensor_copy(ident16[:, :], wt("ident"))
            nc.vector.tensor_copy(triA[:, :], tri_f[:, 0:P])
            nc.vector.tensor_copy(triB[:, :], tri_f[:, P:2 * P])
            xv = X[0][:, :].rearrange("p (t w) -> p t w", w=XW)
            nc.vector.memset(xv[:, :, 0:2], SCALE)
            nc.vector.memset(ones16[:, 2:D + 2], 0.0)
            nc.vector.memset(ones16[:, 0:2], SCALE)
            nc.vector.scalar_tensor_tensor(out=hbias[:, :], in0=wt("w1t"), scalar=wt("t"), in1=wt("b1"),
                                           op0=ALU.mult, op1=ALU.add).then_inc(const_ready, 1)
            sweep_steps(dve, step, finish)

        @block.tensor
        def _(pe):
            def nat_free(n):
                if not (isinstance(n, int) and n == 0):
                    pe.wait_ge(nat_evac, n)

            def tr_free(n):
                if not (isinstance(n, int) and n == 0):
                    pe.wait_ge(tr_evac, n)

            def acc_ordinal(p, c):
                return NC * p + c

            def epilogue(at, e):
                p, c, par = e
                if at == 0 and p in (L1A, L1B):
                    n = tr_no(p, c, 0)
                    tr_free(n)
                    x = X[p % 2]
                    for j in range(4):
                        last = nc.tensor.transpose(tr[:, j * D:(j + 1) * D].bitcast(F16),
                                                   x[:, bass.ds(c * (4 * XW) + j * XW + 2, 2 * D)], ident16[:, :])
                    last.then_inc(tr_done, 1)
                if at == 1:
                    n = nat_no(p, c, 0)
                    nat_free(n)
                    pe.wait_ge(acc_evac, acc_ordinal(p, c) + 1)
                    if p == L0:
                        pe.wait_ge(accb_evac, c + 1)
                        for j in range(4):
                            o = nat[:, j * (D + 1):(j + 1) * (D + 1)]
                            nc.tensor.matmul(o, accS[:, j * P:(j + 1) * P], wt("joinA"), start=True, stop=False)
                            last = nc.tensor.matmul(o, accBS[0:D + 2, j * P:(j + 1) * P], wt("joinB", D + 2),
                                                    start=False, stop=True)
                    elif p in (L1A, L1B):
                        pe.wait_ge(tr_evac, tr_no(p, c, 0) + 1)
                        k = 0 if p == L1A else 1
                        for j in range(4):
                            o = nat[:, j * D:(j + 1) * D]
                            nc.tensor.matmul(o, accS[:, j * P:(j + 1) * P], wt(f"wagg{k}"), start=True, stop=False)
                            last = nc.tensor.matmul(o, accBS[:, j * P:(j + 1) * P], wt(f"wx{k}"),
                                                    start=False, stop=True)
                    else:
                        for j in range(4):
                            last = nc.tensor.matmul(nat[:, j * D:(j + 1) * D], accS[:, j * P:(j + 1) * P],
                                                    wt("joinA", P, 0, D), start=True, stop=True)
                    last.then_inc(nat_done, 1)
                if at == 4 and p in (L1B, L2):
                    n = tr_no(p, c, 1 if p == L1B else 0)
                    tr_free(n)
                    pe.wait_ge(h_ready, 8 * (p - L1B) + c + 1)
                    for j in range(4):
                        last = nc.tensor.matmul(tr[0:D, j * P:(j + 1) * P], hS[:, j * D:(j + 1) * D], wt("ident"),
                                                start=True, stop=True)
                    last.then_inc(tr_done, 1)
                if at == 5 and p in (L1B, L2):
                    n = nat_no(p, c, 1)
                    nat_free(n)
                    pe.wait_ge(tr_evac, tr_no(p, c, 1 if p == L1B else 0) + 1)
                    w = wt("l2w" if p == L1B else "bT", D)
                    for j in range(4):
                        last = nc.tensor.matmul(nat[:, j * D:(j + 1) * D], accBS[0:D, j * P:(j + 1) * P], w,
                                                start=True, stop=True)
                    last.then_inc(nat_done, 1)
                if at in (5, 6) and p == L2:
                    h = at - 5
                    n = tr_no(p, c, 1 + h)
                    tr_free(n)
                    nc.tensor.matmul(tr[:, :], wt("w1", D, h * P, (h + 1) * P), accBS[0:D, :], start=True, stop=True)\
                        .then_inc(tr_done, 1)
                if at == 7 and p == L2:
                    n = nat_no(p, c, 2)
                    nat_free(n)
                    pe.wait_ge(tr_evac, tr_no(p, c, 2) + 1)
                    for j in range(4):
                        for h in range(2):
                            last = nc.tensor.matmul(nat[:, j * D:(j + 1) * D],
                                                    hidS[:, h * W + j * P:h * W + (j + 1) * P],
                                                    wt("w2", P, h * D, (h + 1) * D), start=(h == 0), stop=(h == 1))
                    last.then_inc(nat_done, 1)

            def main(p, c, par, b):
                x = X[p % 2]
                if p == L2:
                    for pair in (2 * b, 2 * b + 1):
                        triangle(c, pair)
                        if pair >= 2:
                            weigh(c, par, pair - 2)
                    return
                q = b
                inring = q in RINGED
                if q in loaded(p):
                    pe.wait_ge(split_ready, split_no(p, c, q) + 1)
                if isinstance(c, int) and c == 0:
                    if p == L3:
                        pe.wait_ge(nat_used, nat_no(L2, q, 1) + 1)
                    else:
                        pe.wait_ge(x_ready, q // 2 + 1 if p == L0 else PRO_GROUPS + NC * (p - 1) + q + 1)
                for k in range(TQ):
                    t = TQ * q + k
                    first, end = t == 0, t == NT - 1
                    if inring:
                        hi, lo = (ringed(RINGED.index(q), part, k, 1) for part in range(2))
                    else:
                        hi, lo = (cached(c, q, part, k, 1) for part in range(2))
                    acc = accA[:, par, :]
                    both = tile(x, t, 2, 2 * D)
                    nc.tensor.matmul(acc, both, hi, start=first, stop=end and p == L0)
                    if p == L0:
                        accb = spare[0:D + 2, par, :]
                        nc.tensor.matmul(accb, tile(x, t, 0, D + 2), lo, start=first, stop=False)
                        last = nc.tensor.matmul(accb, ones16[:, :], hi, start=False, stop=end)
                    else:
                        last = nc.tensor.matmul(acc, both, lo, start=False, stop=end)
                if inring:
                    last.then_inc(ring_done, 1)

            def triangle(c, pair):
                pe.wait_ge(u_ready, NT * c + 2 * pair + 2)
                if pair >= 2 or not (isinstance(c, int) and c == 0):
                    pe.wait_ge(w_ready, 16 * c + pair - 1)
                for i in range(2):
                    t = 2 * pair + i
                    o = spare[:, 2 * (pair % 2) + i, :]
                    last = nc.tensor.matmul(o, triA[:, :], uS[:, (t % 8) * W:(t % 8 + 1) * W],
                                            start=True, stop=(t == 0))
                    if t:
                        last = nc.tensor.matmul(o, triB[:, :], uS[:, ((t - 1) % 8) * W:((t - 1) % 8 + 1) * W],
                                                start=False, stop=True)
                last.then_inc(tri_done, 1)

            def weigh(c, par, pair):
                pe.wait_ge(w_ready, 16 * c + pair + 1)
                for i in range(2):
                    t = 2 * pair + i
                    w = wS[:, ((pair % 4) * 2 + i) * W:((pair % 4) * 2 + i + 1) * W].bitcast(BF16)
                    last = nc.tensor.matmul(accA[:, par, :], tile(X[L2 % 2], NT - 1 - t, 2, 2 * D), w,
                                            start=(t == 0), stop=(t == NT - 1))
                last.then_inc(w_used, 1)

            def step(p, c, par, before):
                early = p == L2 and isinstance(c, int) and c == 0
                if early:
                    for b in range(NQ):
                        epilogue(b, before)
                    pe.wait_ge(nat_used, nat_no(L1B, NC - 1, 1) + 1)
                s = NC * p + c
                if not (isinstance(c, int) and c < 2 and p == L0):
                    pe.wait_ge(acc_evac, s - 1)
                    if p == L0:
                        pe.wait_ge(accb_evac, s - 1)
                for b in range(NQ):
                    main(p, c, par, b)
                    if before and not early:
                        epilogue(b, before)
                if p == L2:
                    weigh(c, par, 14)
                    weigh(c, par, 15)

            def finish(before):
                for b in range(NQ):
                    epilogue(b, before)

            pe.wait_ge(const_ready, 1)
            sweep_steps(pe, step, finish)


def kernel(x, adj, L0_gnn_t, L1_gnn_W, L2_gnn_weight, L2_gnn_bias, L3_gnn_t, L3_gnn_B, L3_gnn_W1,
           L3_gnn_b1, L3_gnn_W2, L3_gnn_b2):
    import concourse.bacc as bacc
    from concourse.bass_utils import run_bass_kernel_spmd

    def host(a):
        return np.asarray(a)

    x_rows = np.ascontiguousarray(host(x).reshape(NT, P, D).transpose(1, 0, 2)).reshape(P, NT * D)
    blocks = np.ascontiguousarray(host(adj).reshape(NC, W, NQ, TQ, P).transpose(0, 2, 4, 3, 1))
    blocks = blocks.reshape(NC * NQ * P, BLK)

    wts = np.zeros((P, NCOLS), np.float32)

    def put(name, a):
        lo, hi = COLS[name]
        wts[0:a.shape[0], lo:hi] = a

    for k in range(2):
        for h in range(2):
            lo, hi = COLS[f"wagg{k}"]
            wts[h * D:(h + 1) * D, lo:hi] = host(L1_gnn_W)[k, 0:D]
            lo, hi = COLS[f"wx{k}"]
            wts[h * D:(h + 1) * D, lo:hi] = host(L1_gnn_W)[k, D:2 * D]
    put("l2w", host(L2_gnn_weight))
    put("bT", host(L3_gnn_B).T)
    put("w1", host(L3_gnn_W1)[0:D])
    put("w2", host(L3_gnn_W2).reshape(2, P, D).transpose(1, 0, 2).reshape(P, 2 * D))
    put("w1t", host(L3_gnn_W1)[D].reshape(2, P).T)
    put("b1", host(L3_gnn_b1).reshape(2, P).T)
    put("t", np.broadcast_to(host(L3_gnn_t).reshape(1, 1), (P, 1)))
    put("bias", np.broadcast_to(host(L2_gnn_bias).reshape(1, D), (P, D)))
    put("b2", np.broadcast_to(host(L3_gnn_b2).reshape(1, D), (P, D)))
    put("ident", np.eye(P, dtype=np.float32))
    eye = np.eye(D, dtype=np.float32)
    put("joinA", np.concatenate([np.concatenate([eye, eye], 0), np.zeros((P, 1), np.float32)], 1))
    join_b = np.zeros((P, D + 1), np.float32)
    join_b[2:2 + D, 0:D] = eye
    join_b[0, D] = 1.0
    put("joinB", join_b)
    i, j = np.arange(P)[:, None], np.arange(P)[None, :]
    tri_a = np.where(i > j, -BIT, np.where(i == j, NEIGH * BIT, 0.0)).astype(np.float32)
    tri_b = np.float32(-BIT) - tri_a
    tri = np.concatenate([tri_a, tri_b], 1)

    nc = bacc.Bacc("TRN2", target_bir_lowering=False, num_devices=1)
    arrays = {"x_rows": x_rows, "adj_blocks": blocks, "weights": wts, "triangles": tri}
    args = [nc.dram_tensor(n, a.shape, mybir.dt.from_np(a.dtype), kind="ExternalInput").ap()
            for n, a in arrays.items()]
    out = nc.dram_tensor("out_rows", (P, NT * D), F32, kind="ExternalOutput").ap()
    gnn_kernel(nc, *args, out)
    r = run_bass_kernel_spmd(nc, [arrays], core_ids=[0])
    got = r.results[0]["out_rows"]
    return np.ascontiguousarray(got.reshape(P, NT, D).transpose(1, 0, 2)).reshape(N, D)
```

```python
from contextlib import ExitStack

import numpy as np

import concourse.bass as bass
from concourse import mybir

ALU = mybir.AluOpType
ACT = mybir.ActivationFunctionType
AX_X = mybir.AxisListType.X
F32 = mybir.dt.float32
F16 = mybir.dt.float16
BF16 = mybir.dt.bfloat16
U16 = mybir.dt.uint16

P = 128
N = 4096
D = 64
NT = N // P
W = 512
NC = N // W
TQ = 2
NQ = NT // TQ
BLK = TQ * W
EPS = 1e-5
PRO_GROUPS = 4

L0, L1A, L1B, L2, L3 = range(5)
SPLIT_SWEEPS = (L0, L1A, L1B, L3)
CACHED = tuple(range(0, NQ, 4))
RINGED = tuple(q for q in range(NQ) if q % 4)
NR = len(RINGED)
LAND = 8
LANDR = 6
RING = 4

SCALE = 4096.0
UNSCALE = 1.0 / (SCALE * SCALE)
NEIGH = 100
BIT = 128.0
L2_UNSCALE = 2.0 ** (127 - NEIGH) / SCALE
XW = 2 * D + 2

COLS = {}
_at = 0
for _name, _n in (("wagg0", D), ("wx0", D), ("wagg1", D), ("wx1", D), ("l2w", D), ("bT", D), ("w1", 256),
                  ("w2", 2 * D), ("w1t", 2), ("b1", 2), ("t", 1), ("bias", D), ("b2", D),
                  ("ident", P), ("joinA", D + 1), ("joinB", D + 1)):
    COLS[_name] = (_at, _at + _n)
    _at += _n
NCOLS = _at
LN_STEPS = 5
EPI_LINKS = {L0: 4 + LN_STEPS, L1A: 0, L1B: LN_STEPS, L2: LN_STEPS, L3: LN_STEPS + 5}


def loaded(p):
    if p == L0:
        return list(range(NQ))
    return list(reversed(RINGED)) if p == L2 else list(RINGED)


def slot_use(p, s, q):
    first = q < LAND if p != L2 else q >= LAND
    return 2 * s + (0 if first else 1)


def split_no(p, c, q):
    if p == L0:
        return NQ * c + q
    before = {L1A: 0, L1B: 1, L3: 2}[p]
    return NQ * NC + NR * NC * before + NR * c + RINGED.index(q)


def ring_no(p, c, q):
    return NR * (NC * SPLIT_SWEEPS.index(p) + c) + RINGED.index(q)


def nat_no(p, c, i=0):
    return {L0: c, L1A: 8 + c, L1B: 16 + 2 * c + i, L2: 32 + 2 * c + i, L3: 48 + 2 * c + i}[p]


def tr_no(p, c, i=0):
    return {L1A: c, L1B: 8 + 2 * c + i, L2: 24 + c, L3: 32 + 3 * c + i}[p]


def row_no(p, c):
    return {L0: c, L1B: 8 + c, L2: 16 + c, L3: 24 + c}[p]


def ready_no(p, c):
    return {L0: 0, L2: NC}[p] + c


def h_no(p, c):
    return {L0: 0, L1B: NC, L2: 2 * NC, L3: 3 * NC}[p] + c


def x_no(p, c):
    return NC * p + c


def norm_no(p, c):
    return PRO_GROUPS + {L0: 0, L1B: NC, L2: 2 * NC, L3: 3 * NC}[p] + c


def link_base(p, c):
    return PROLOGUE_LINKS + sum(NC * EPI_LINKS[k] for k in range(p)) + EPI_LINKS[p] * c


PROLOGUE_LINKS = PRO_GROUPS * (LN_STEPS + 2)


HT_ACT = {L0: None, L1A: None, L1B: 6, L2: 6, L3: 5}
HT_PE = {L0: None, L1A: None, L1B: 5, L2: 5, L3: 4}


def sweep_steps(eng, step, finish):
    for p in range(5):
        step(p, 0, 0, (p - 1, NC - 1, 1) if p else None)
        start = 1
        if p == L0:
            step(p, 1, 1, (p, 0, 0))
            step(p, 2, 0, (p, 1, 1))
            start = 3
        with eng.Fori(start, NC - 1, 2) as c:
            step(p, c, 1, (p, c - 1, 0))
            step(p, c + 1, 0, (p, c, 1))
        step(p, NC - 1, 1, (p, NC - 2, 0))
    finish((L3, NC - 1, 1))


def gnn_kernel(nc, x_in, adj_in, wts_in, tri_in, out):
    x1_d = nc.dram_tensor("x1_rows", (P, NT * D), F32, kind="Internal").ap()
    x2_d = nc.dram_tensor("x2_rows", (P, NT * D), F32, kind="Internal").ap()
    x3_d = nc.dram_tensor("x3_rows", (P, NT * D), F32, kind="Internal").ap()
    rows_from = {L0: x_in, L1B: x1_d, L2: x2_d, L3: x3_d}
    rows_to = {L0: x1_d, L1B: x2_d, L2: x3_d, L3: out}

    with ExitStack() as ctx:
        def sb(name, shape, dt):
            return ctx.enter_context(nc.sbuf_tensor(name, shape, dt))

        def psum(name, shape, dt):
            return ctx.enter_context(nc.psum_tensor(name, shape, dt))

        def sem(name):
            return ctx.enter_context(nc.semaphore(name))

        cache = sb("cache", [P, NC * len(CACHED) * 2 * BLK], F16)
        ring = sb("ring", [P, RING, 2 * BLK], F16)
        land = sb("land", [P, LAND, BLK], F32)
        X = [sb(f"X{i}", [P, NT * XW], F16) for i in range(2)]
        wts = sb("wts", [P, NCOLS], F32)
        ident16 = sb("ident16", [P, P], F16)
        ones16 = sb("ones16", [P, D + 2], F16)
        triA = sb("triA", [P, P], BF16)
        triB = sb("triB", [P, P], BF16)
        accS = sb("accS", [P, W], F32)
        accBS = sb("accBS", [P, W], F32)
        natS = sb("natS", [P, 4 * (D + 1)], F32)
        xin = sb("xin", [P, 4 * D], F32)
        zS = sb("zS", [P, 4 * D], F32)
        tS = sb("tS", [P, 4 * D], F32)
        hS = sb("hS", [P, 4 * D], F32)
        rowsum = sb("rowsum", [P, NT], F32)
        st = sb("st", [P, 16], F32)
        var = sb("var", [P, 8], F32)
        rstd = sb("rstd", [P, 8], F32)
        power = sb("power", [P, 8], F32)
        scale = sb("scale", [P, 1], F32)
        hbias = sb("hbias", [P, 2], F32)
        uS = ring[:, 0:2, :].rearrange("p a n -> p (a n)").bitcast(BF16)
        wS = ring[:, 2:4, :].rearrange("p a n -> p (a n)")
        hidS = land[:, 0, :]
        yS = land[:, 4, 0:4 * D]
        x_all = cache[:, 15 * NT * P:16 * NT * P].bitcast(F32)
        pro = cache[:, 14 * NT * P:15 * NT * P].bitcast(F32)
        tri_f = cache[:, 13 * NT * P:14 * NT * P].bitcast(F32)

        accA = psum("accA", [P, 2, W], F32)
        spare = psum("spare", [P, 4, W], F32)
        nat = psum("nat", [P, W], F32)
        tr = psum("tr", [P, W], F32)

        landed = [sem(f"landed{i}") for i in range(LAND)]
        wts_in_s, tri_in_s, x_in_s = sem("wts_in"), sem("tri_in"), sem("x_in")
        hi_ready = sem("hi_ready")
        split_ready = sem("split_ready")
        ring_done = sem("ring_done")
        acc_evac, accb_evac = sem("acc_evac"), sem("accb_evac")
        nat_done, nat_evac, nat_used = sem("nat_done"), sem("nat_evac"), sem("nat_used")
        tr_done, tr_evac = sem("tr_done"), sem("tr_evac")
        h_ready = sem("h_ready")
        x_ready = sem("x_ready")
        hi_rows = sem("hi_rows")
        link = sem("link")
        const_ready = sem("const_ready")
        rows_in, rows_out = sem("rows_in"), sem("rows_out")
        rows_used, rows_ready = sem("rows_used"), sem("rows_ready")
        var_ready, rstd_ready = sem("var_ready"), sem("rstd_ready")
        power_ready = sem("power_ready")
        u_ready = sem("u_ready")
        tri_done = sem("tri_done")
        w_ready = sem("w_ready")
        w_used = sem("w_used")

        def wt(name, rows=P, lo=0, hi=None):
            a, b = COLS[name]
            return wts[0:rows, a + lo:(b if hi is None else a + hi)]

        def chunk_tiles(x, c, lo, n):
            v = x[:, bass.ds(c * (4 * XW), 4 * XW)].rearrange("p (t w) -> p t w", w=XW)
            return v[:, :, lo:lo + n]

        def tile(x, t, lo, n):
            return x[:, t * XW + lo:t * XW + lo + n]

        def cached(c, q, part, k=0, n=TQ):
            return cache[:, bass.ds(c * (len(CACHED) * 2 * BLK) + ((q // 4) * 2 + part) * BLK + k * W, n * W)]

        def ringed(r, part, k=0, n=TQ):
            return ring[:, r % RING, part * BLK + k * W:part * BLK + (k + n) * W]

        def rows4(t):
            return t[:, 0:4 * D].rearrange("p (t d) -> p t d", d=D)

        def spread(col):
            return col.rearrange("p (t o) -> p t o", o=1).to_broadcast([P, col.shape[1], D])

        def over_tiles(name):
            return wt(name).rearrange("p (o d) -> p o d", o=1).to_broadcast([P, 4, D])

        block = ctx.enter_context(nc.Block())

        @block.sync
        def _(sp):
            sp.dma_start(x_all, x_in).then_inc(x_in_s, 16)
            sp.dma_start(wts[:, :], wts_in).then_inc(wts_in_s, 16)
            sp.dma_start(tri_f[:, 0:2 * P], tri_in).then_inc(tri_in_s, 16)

            def step(p, c, par, before):
                qs = loaded(p)
                for i, q in enumerate(qs):
                    if p == L0:
                        if i >= LAND:
                            sp.wait_ge(split_ready, split_no(p, c, q - LAND) + 1)
                        elif not (isinstance(c, int) and c == 0):
                            sp.wait_ge(split_ready, split_no(p, c - 1, q + LAND) + 1)
                    else:
                        if i >= LANDR:
                            pp, pc, pq = p, c, qs[i - LANDR]
                        elif isinstance(c, int) and c == 0:
                            pp, pc = p - 1, NC - 1
                            pq = [b for b in loaded(pp) if b % LAND == q % LAND][-1]
                        else:
                            pp, pc, pq = p, c - 1, qs[i + LANDR]
                        if pp == L2:
                            sp.wait_ge(u_ready, NT * pc + NT - TQ * pq)
                        else:
                            sp.wait_ge(split_ready, split_no(pp, pc, pq) + 1)
                    sp.dma_start(land[:, q % LAND, :], adj_in[bass.ds(c * (NQ * P) + q * P, P), :])\
                        .then_inc(landed[q % LAND], 16)

            sweep_steps(sp, step, lambda before: None)

        @block.gpsimd
        def _(pool):
            def inverse_root(number, ntile):
                pool.wait_ge(var_ready, number + 1)
                nc.gpsimd.tensor_tensor(rstd[:, 0:ntile], var[:, 0:ntile], power[:, 0:ntile], ALU.pow)\
                    .then_inc(rstd_ready, 1)

            def split_rows(p, c):
                nxt = X[(p + 1) % 2]
                hi, lo = chunk_tiles(nxt, c, 2, D), chunk_tiles(nxt, c, 2 + D, D)
                if p == L0:
                    pool.wait_ge(h_ready, h_no(p, c) + 1)
                    v = rows4(hS)
                elif p == L1A:
                    pool.wait_ge(x_ready, PRO_GROUPS + x_no(p, c))
                    pool.wait_ge(nat_evac, nat_no(p, c, 0) + 1)
                    nc.gpsimd.tensor_tensor(yS[:, :], natS[:, 0:4 * D], scale[:, 0:1].to_broadcast([P, 4 * D]), ALU.mult)\
                        .then_inc(nat_used, 1)
                    pool.wait_ge(nat_used, nat_no(p, c, 0) + 1)
                    v = rows4(yS)
                else:
                    pool.wait_ge(nat_evac, nat_no(p, c, 1) + 1)
                    v = rows4(natS)
                nc.gpsimd.tensor_copy(hi, v).then_inc(hi_rows, 1)
                pool.wait_ge(hi_rows, x_no(p, c) + 1)
                nc.gpsimd.tensor_tensor(lo, v, hi, ALU.subtract)\
                    .then_inc(x_ready if p in (L0, L1A) else nat_used, 1)

            def epilogue(e):
                p, c, par = e
                if p != L1A:
                    inverse_root(norm_no(p, c), 4)
                if p != L3:
                    split_rows(p, c)

            def step(p, c, par, before):
                if before:
                    epilogue(before)

            nc.gpsimd.memset(power[:, :], -0.5).then_inc(power_ready, 1)
            nc.gpsimd.memset(scale[:, :], SCALE).then_inc(power_ready, 1)
            pool.wait_ge(power_ready, 2)
            for g in range(PRO_GROUPS):
                inverse_root(g, 8)
            sweep_steps(pool, step, epilogue)

        @block.scalar
        def _(act):
            def xin_read(p, c):
                if p == L0:
                    act.wait_ge(rows_used, c + 1)
                else:
                    act.wait_ge(nat_used, nat_no(p, c, 0) + 1)

            def epilogue(at, e):
                p, c, par = e
                if at == 0 and p in rows_from:
                    if not (isinstance(c, int) and c == 0):
                        xin_read(p, c - 1)
                    elif p != L0:
                        xin_read({L1B: L0, L2: L1B, L3: L2}[p], NC - 1)
                    act.dma_start(xin[:, :], rows_from[p][:, bass.ds(c * (4 * D), 4 * D)]).then_inc(rows_in, 16)
                if at == 1:
                    if p == L2:
                        act.wait_ge(w_used, 16 * (c + 1))
                    else:
                        act.wait_ge(ring_done, ring_no(p, c, NQ - 1) + 1)
                    if not (isinstance(c, int) and c == 0 and p == L0):
                        act.wait_ge(nat_done, nat_no(p, c, 0))
                    nc.scalar.activation(accS[:, :], accA[:, par, :], ACT.Copy,
                                         scale=L2_UNSCALE if p == L2 else UNSCALE).then_inc(acc_evac, 1)
                    if p == L0:
                        nc.scalar.activation(accBS[0:D + 2, :], spare[0:D + 2, par, :], ACT.Copy, scale=UNSCALE)\
                            .then_inc(accb_evac, 1)
                    if p in (L1A, L1B):
                        act.wait_ge(tr_done, tr_no(p, c, 0) + 1)
                        nc.scalar.activation(accBS[:, :], tr[:, 0:W // 2].bitcast(F16), ACT.Copy, scale=1.0 / SCALE)\
                            .then_inc(tr_evac, 1)
                if at == 3:
                    n = nat_no(p, c, 0)
                    act.wait_ge(nat_done, n + 1)
                    if not (isinstance(n, int) and n == 0):
                        act.wait_ge(nat_used, n)
                    width = 4 * (D + 1) if p == L0 else 4 * D
                    nc.scalar.activation(natS[:, 0:width], nat[:, 0:width],
                                         ACT.Tanh if p in (L1A, L1B) else ACT.Copy).then_inc(nat_evac, 1)
                if at == HT_ACT[p]:
                    i = 1 if p == L1B else 0
                    act.wait_ge(tr_done, tr_no(p, c, i) + 1)
                    nc.scalar.activation(accBS[0:D, :], tr[0:D, :], ACT.Copy).then_inc(tr_evac, 1)
                if at == 7 and p in (L1B, L2):
                    n = nat_no(p, c, 1)
                    act.wait_ge(nat_done, n + 1)
                    act.wait_ge(nat_used, n)
                    nc.scalar.activation(natS[:, 0:4 * D], nat[:, 0:4 * D], ACT.Copy, scale=SCALE)\
                        .then_inc(nat_evac, 1)
                if p == L3 and at in (6, 7):
                    h = at - 6
                    act.wait_ge(tr_done, tr_no(p, c, 1 + h) + 1)
                    nc.scalar.activation(hidS[:, h * W:(h + 1) * W], tr[:, :], ACT.Tanh, bias=hbias[:, h:h + 1])\
                        .then_inc(tr_evac, 1)
                if p == L3 and at == 7:
                    n = nat_no(p, c, 1)
                    act.wait_ge(nat_done, n + 1)
                    act.wait_ge(nat_used, n)
                    nc.scalar.activation(natS[:, 0:4 * D], nat[:, 0:4 * D], ACT.Copy).then_inc(nat_evac, 1)
                if at == 7 and p in rows_to:
                    if p == L1B:
                        act.wait_ge(nat_used, nat_no(p, c, 0) + 1)
                    elif p == L3:
                        act.wait_ge(nat_used, nat_no(p, c, 1) + 1)
                    else:
                        act.wait_ge(rows_ready, ready_no(p, c) + 1)
                    act.dma_start(rows_to[p][:, bass.ds(c * (4 * D), 4 * D)], zS[:, :]).then_inc(rows_out, 16)

            def main(p, c, par, b):
                if p == L2:
                    pair = b
                    act.wait_ge(tri_done, 16 * c + pair + 1)
                    if pair >= 4 or not (isinstance(c, int) and c == 0):
                        act.wait_ge(w_used, 16 * c + pair - 3)
                    k = pair % 2
                    nc.scalar.activation(wS[:, (pair % 4) * 2 * W:(pair % 4 + 1) * 2 * W].bitcast(U16),
                                         spare[:, 2 * k:2 * k + 2, :].rearrange("p a b -> p (a b)"), ACT.Relu)\
                        .then_inc(w_ready, 1)
                    return
                q = b
                if q not in loaded(p):
                    return
                s = NC * p + c
                act.wait_ge(landed[q % LAND], (slot_use(p, s, q) + 1) * 16)
                if p == L0 and q in CACHED:
                    hi = cached(c, q, 0)
                else:
                    n = ring_no(p, c, q)
                    if not (isinstance(n, int) and n < RING):
                        act.wait_ge(ring_done, n - RING + 1)
                    if p == L3 and isinstance(c, int) and c == 0 and q == RINGED[2]:
                        act.wait_ge(w_used, 16 * NC)
                    hi = ringed(RINGED.index(q), 0)
                nc.scalar.activation(hi, land[:, q % LAND, :], ACT.Copy, scale=SCALE).then_inc(hi_ready, 1)

            def step(p, c, par, before):
                early = p == L2 and isinstance(c, int) and c == 0
                if early:
                    for at in range(8):
                        epilogue(at, before)
                for b in range(NQ):
                    main(p, c, par, b)
                    if b % 2 and before and not early:
                        epilogue(b // 2, before)

            def finish(before):
                for at in range(8):
                    epilogue(at, before)
                act.wait_ge(rows_out, 16 * 4 * NC)

            act.wait_ge(const_ready, 1)
            sweep_steps(act, step, finish)

        @block.vector
        def _(dve):
            class Links:
                def __init__(self, base):
                    self.base, self.n = base, 0

                def wait(self):
                    dve.wait_ge(link, self.base + self.n)

                def __call__(self, ins):
                    ins.then_inc(link, 1)
                    self.n += 1
                    self.wait()

            def centre(L, z, t, s0, ntile):
                zv, tv, qv = (a.rearrange("p (t d) -> p t d", d=D) for a in (z, t, s0))
                L(nc.vector.tensor_reduce(st[:, 0:ntile], zv, AX_X, ALU.add))
                L(nc.vector.scalar_tensor_tensor(out=tv, in0=spread(st[:, 0:ntile]), scalar=-1.0 / D, in1=zv,
                                                 op0=ALU.mult, op1=ALU.add))
                L(nc.vector.tensor_tensor(qv, tv, tv, ALU.mult))

            def variance(L, s0, ntile):
                L(nc.vector.tensor_reduce(st[:, 8:8 + ntile], s0.rearrange("p (t d) -> p t d", d=D), AX_X, ALU.add))
                nc.vector.tensor_scalar(var[:, 0:ntile], st[:, 8:8 + ntile], D * EPS, None, ALU.add)\
                    .then_inc(var_ready, 1)

            def norm_relu(L, t, h, ntile, number, scale):
                tv = t.rearrange("p (t d) -> p t d", d=D)
                dve.wait_ge(rstd_ready, number + 1)
                L(nc.vector.tensor_tensor(tv, tv, spread(rstd[:, 0:ntile]), ALU.mult))
                return nc.vector.tensor_scalar(h, t, 0.0, scale * float(np.sqrt(D)), ALU.max, ALU.mult)

            links = {}

            def epilogue(at, e):
                p, c, par = e
                if at == 0:
                    links[0] = Links(link_base(p, c))
                L = links[0]
                n0 = nat_no(p, c, 0)
                if p == L1A:
                    return
                k = row_no(p, c)

                def sums_in():
                    dve.wait_ge(nat_evac, n0 + 1)

                def rows_in_sbuf():
                    dve.wait_ge(rows_in, (k + 1) * 16)

                def rows_written():
                    if not (isinstance(k, int) and k == 0):
                        dve.wait_ge(rows_out, k * 16)

                if p == L0:
                    n5 = natS[:, 0:4 * (D + 1)].rearrange("p (t d) -> p t d", d=D + 1)
                    here = X[L0 % 2]
                    if at == 3:
                        sums_in()
                        if not (isinstance(c, int) and c == 0):
                            dve.wait_ge(x_ready, PRO_GROUPS + c)
                        L(nc.vector.tensor_tensor(rows4(hS), chunk_tiles(here, c, 2, D),
                                                  chunk_tiles(here, c, 2 + D, D), ALU.add))
                        L(nc.vector.tensor_tensor(rows4(tS), rows4(hS), n5[:, :, 0:D], ALU.mult))
                        L(nc.vector.tensor_reduce(st[:, 0:4], rows4(tS), AX_X, ALU.add))
                        nc.vector.tensor_copy(rowsum[:, bass.ds(c * 4, 4)].rearrange("p (t o) -> p t o", o=1),
                                              n5[:, :, D:D + 1]).then_inc(nat_used, 1)
                    if at == 4:
                        L(nc.vector.tensor_scalar(st[:, 8:12], st[:, 0:4], -0.01 / SCALE, 1.0, ALU.mult, ALU.add))
                        rows_in_sbuf()
                        rows_written()
                        nc.vector.scalar_tensor_tensor(out=tS[:, :], in0=hS[:, :], scalar=-0.1 / SCALE,
                                                       in1=xin[:, :], op0=ALU.mult, op1=ALU.add).then_inc(rows_used, 1)
                        dve.wait_ge(rows_used, k + 1)
                        nc.vector.tensor_tensor(rows4(zS), rows4(tS), spread(st[:, 8:12]), ALU.add)\
                            .then_inc(rows_ready, 1)
                    if at == 5:
                        dve.wait_ge(rows_ready, ready_no(p, c) + 1)
                        centre(L, zS[:, :], tS[:, :], hS[:, :], 4)
                    if at == 6:
                        variance(L, hS[:, :], 4)
                    if at == 7:
                        norm_relu(L, tS[:, :], hS[:, :], 4, norm_no(p, c), SCALE).then_inc(h_ready, 1)
                elif p in (L1B, L2):
                    if at == 3:
                        sums_in()
                        rows_in_sbuf()
                        rows_written()
                        new = zS if p == L1B else tS
                        nc.vector.tensor_tensor(new[:, :], xin[:, :], natS[:, 0:4 * D], ALU.add).then_inc(nat_used, 1)
                        dve.wait_ge(nat_used, n0 + 1)
                        if p == L2:
                            nc.vector.tensor_tensor(rows4(zS), rows4(tS), over_tiles("bias"), ALU.add)\
                                .then_inc(rows_ready, 1)
                            dve.wait_ge(rows_ready, ready_no(p, c) + 1)
                        centre(L, zS[:, :], tS[:, :], hS[:, :], 4)
                    if at == 4:
                        variance(L, hS[:, :], 4)
                    if at == 5:
                        norm_relu(L, tS[:, :], hS[:, :], 4, norm_no(p, c), 1.0).then_inc(h_ready, 1)
                else:
                    if at == 1:
                        rows_in_sbuf()
                        dve.wait_ge(tr_evac, tr_no(p, c, 0))
                        centre(L, xin[:, :], tS[:, :], hS[:, :], 4)
                    if at == 2:
                        variance(L, hS[:, :], 4)
                    if at == 3:
                        norm_relu(L, tS[:, :], hS[:, :], 4, norm_no(p, c), 1.0).then_inc(h_ready, 1)
                    if at == 4:
                        here = X[L3 % 2]
                        L(nc.vector.tensor_scalar(st[:, 0:4], rowsum[:, bass.ds(c * 4, 4)], -1.0 / SCALE, None,
                                                  ALU.mult))
                        L(nc.vector.tensor_tensor(rows4(tS), chunk_tiles(here, c, 2, D),
                                                  chunk_tiles(here, c, 2 + D, D), ALU.add))
                        L(nc.vector.tensor_tensor(rows4(yS), rows4(tS), spread(st[:, 0:4]), ALU.mult))
                        sums_in()
                        nc.vector.tensor_tensor(tS[:, :], xin[:, :], natS[:, 0:4 * D], ALU.add).then_inc(nat_used, 1)
                        dve.wait_ge(nat_used, n0 + 1)
                        L(nc.vector.tensor_tensor(tS[:, :], tS[:, :], yS[:, :], ALU.add))
                        L(nc.vector.tensor_tensor(rows4(yS), rows4(tS), over_tiles("b2"), ALU.add))
                    if at == 7:
                        rows_written()
                        dve.wait_ge(nat_evac, nat_no(p, c, 1) + 1)
                        nc.vector.tensor_tensor(zS[:, :], yS[:, :], natS[:, 0:4 * D], ALU.add).then_inc(nat_used, 1)

            def main(p, c, par, b):
                if p == L2:
                    q = NQ - 1 - b
                    if q not in CACHED:
                        dve.wait_ge(landed[q % LAND], (slot_use(p, NC * p + c, q) + 1) * 16)
                    for i in range(TQ):
                        k = TQ - 1 - i
                        t = TQ * b + i
                        src = cached(c, q, 0, k, 1) if q in CACHED else land[:, q % LAND, k * W:(k + 1) * W]
                        u = uS[:, (t % 8) * W:(t % 8 + 1) * W]
                        if t >= 8 or not (isinstance(c, int) and c == 0):
                            dve.wait_ge(tri_done, 16 * c + (t - 7) // 2 + 1)
                        if t == 0:
                            nc.vector.tensor_scalar(u, src, 0.0, None, ALU.not_equal).then_inc(u_ready, 1)
                        else:
                            dve.wait_ge(u_ready, NT * c + t)
                            prev = uS[:, ((t - 1) % 8) * W:((t - 1) % 8 + 1) * W]
                            nc.vector.scalar_tensor_tensor(out=u, in0=src, scalar=0.0, in1=prev,
                                                           op0=ALU.not_equal, op1=ALU.add).then_inc(u_ready, 1)
                    return
                q = b
                if q not in loaded(p):
                    return
                n = split_no(p, c, q)
                dve.wait_ge(hi_ready, n + 1)
                if p == L0 and q in CACHED:
                    hi, lo = cached(c, q, 0), cached(c, q, 1)
                else:
                    hi, lo = ringed(RINGED.index(q), 0), ringed(RINGED.index(q), 1)
                nc.vector.scalar_tensor_tensor(out=lo, in0=land[:, q % LAND, :], scalar=SCALE, in1=hi,
                                               op0=ALU.mult, op1=ALU.subtract).then_inc(split_ready, 1)

            def step(p, c, par, before):
                early = p == L2 and isinstance(c, int) and c == 0
                first = p == L0 and isinstance(c, int) and c == 0
                if early:
                    for at in range(8):
                        epilogue(at, before)
                for b in range(NQ):
                    if first and b % 4 == 0:
                        prologue_group(b // 4)
                    main(p, c, par, b)
                    if b % 2 and before and not early:
                        epilogue(b // 2, before)

            def finish(before):
                for at in range(8):
                    epilogue(at, before)

            def prologue_group(g):
                L = Links(g * (LN_STEPS + 2))
                n = 8 * D
                z, t, s0 = x_all[:, g * n:(g + 1) * n], pro[:, 0:n], pro[:, n:2 * n]
                centre(L, z, t, s0, 8)
                variance(L, s0, 8)
                L(norm_relu(L, t, s0, 8, g, SCALE))
                v = X[0][:, g * 8 * XW:(g + 1) * 8 * XW].rearrange("p (t w) -> p t w", w=XW)
                sv = s0.rearrange("p (t d) -> p t d", d=D)
                L(nc.vector.tensor_copy(v[:, :, 2:2 + D], sv))
                nc.vector.tensor_tensor(v[:, :, 2 + D:2 + 2 * D], sv, v[:, :, 2:2 + D], ALU.subtract)\
                    .then_inc(x_ready, 1)

            dve.wait_ge(wts_in_s, 16)
            dve.wait_ge(tri_in_s, 16)
            dve.wait_ge(x_in_s, 16)
            nc.vector.tensor_copy(ident16[:, :], wt("ident"))
            nc.vector.tensor_copy(triA[:, :], tri_f[:, 0:P])
            nc.vector.tensor_copy(triB[:, :], tri_f[:, P:2 * P])
            xv = X[0][:, :].rearrange("p (t w) -> p t w", w=XW)
            nc.vector.memset(xv[:, :, 0:2], SCALE)
            nc.vector.memset(ones16[:, 2:D + 2], 0.0)
            nc.vector.memset(ones16[:, 0:2], SCALE)
            nc.vector.scalar_tensor_tensor(out=hbias[:, :], in0=wt("w1t"), scalar=wt("t"), in1=wt("b1"),
                                           op0=ALU.mult, op1=ALU.add).then_inc(const_ready, 1)
            sweep_steps(dve, step, finish)

        @block.tensor
        def _(pe):
            def nat_free(n):
                if not (isinstance(n, int) and n == 0):
                    pe.wait_ge(nat_evac, n)

            def tr_free(n):
                if not (isinstance(n, int) and n == 0):
                    pe.wait_ge(tr_evac, n)

            def acc_ordinal(p, c):
                return NC * p + c

            def epilogue(at, e):
                p, c, par = e
                if at == 0 and p in (L1A, L1B):
                    n = tr_no(p, c, 0)
                    tr_free(n)
                    x = X[p % 2]
                    for j in range(4):
                        last = nc.tensor.transpose(tr[:, j * D:(j + 1) * D].bitcast(F16),
                                                   x[:, bass.ds(c * (4 * XW) + j * XW + 2, 2 * D)], ident16[:, :])
                    last.then_inc(tr_done, 1)
                if at == 1:
                    n = nat_no(p, c, 0)
                    nat_free(n)
                    pe.wait_ge(acc_evac, acc_ordinal(p, c) + 1)
                    if p == L0:
                        pe.wait_ge(accb_evac, c + 1)
                        for j in range(4):
                            o = nat[:, j * (D + 1):(j + 1) * (D + 1)]
                            nc.tensor.matmul(o, accS[:, j * P:(j + 1) * P], wt("joinA"), start=True, stop=False)
                            last = nc.tensor.matmul(o, accBS[0:D + 2, j * P:(j + 1) * P], wt("joinB", D + 2),
                                                    start=False, stop=True)
                    elif p in (L1A, L1B):
                        pe.wait_ge(tr_evac, tr_no(p, c, 0) + 1)
                        k = 0 if p == L1A else 1
                        for j in range(4):
                            o = nat[:, j * D:(j + 1) * D]
                            nc.tensor.matmul(o, accS[:, j * P:(j + 1) * P], wt(f"wagg{k}"), start=True, stop=False)
                            last = nc.tensor.matmul(o, accBS[:, j * P:(j + 1) * P], wt(f"wx{k}"),
                                                    start=False, stop=True)
                    else:
                        for j in range(4):
                            last = nc.tensor.matmul(nat[:, j * D:(j + 1) * D], accS[:, j * P:(j + 1) * P],
                                                    wt("joinA", P, 0, D), start=True, stop=True)
                    last.then_inc(nat_done, 1)
                if at == HT_PE[p]:
                    n = tr_no(p, c, 1 if p == L1B else 0)
                    tr_free(n)
                    pe.wait_ge(h_ready, h_no(p, c) + 1)
                    for j in range(4):
                        last = nc.tensor.matmul(tr[0:D, j * P:(j + 1) * P], hS[:, j * D:(j + 1) * D], wt("ident"),
                                                start=True, stop=True)
                    last.then_inc(tr_done, 1)
                if at == 6 and p in (L1B, L2):
                    n = nat_no(p, c, 1)
                    nat_free(n)
                    pe.wait_ge(tr_evac, tr_no(p, c, 1 if p == L1B else 0) + 1)
                    w = wt("l2w" if p == L1B else "bT", D)
                    for j in range(4):
                        last = nc.tensor.matmul(nat[:, j * D:(j + 1) * D], accBS[0:D, j * P:(j + 1) * P], w,
                                                start=True, stop=True)
                    last.then_inc(nat_done, 1)
                if at in (5, 6) and p == L3:
                    h = at - 5
                    n = tr_no(p, c, 1 + h)
                    tr_free(n)
                    nc.tensor.matmul(tr[:, :], wt("w1", D, h * P, (h + 1) * P), accBS[0:D, :], start=True, stop=True)\
                        .then_inc(tr_done, 1)
                if at == 7 and p == L3:
                    n = nat_no(p, c, 1)
                    nat_free(n)
                    pe.wait_ge(tr_evac, tr_no(p, c, 2) + 1)
                    for j in range(4):
                        for h in range(2):
                            last = nc.tensor.matmul(nat[:, j * D:(j + 1) * D],
                                                    hidS[:, h * W + j * P:h * W + (j + 1) * P],
                                                    wt("w2", P, h * D, (h + 1) * D), start=(h == 0), stop=(h == 1))
                    last.then_inc(nat_done, 1)

            def main(p, c, par, b, before):
                x = X[p % 2]
                if p == L2:
                    pair = b
                    triangle(c, pair)
                    if pair >= 2:
                        weigh(c, par, pair - 2)
                    elif before[0] == L2:
                        weigh(before[1], before[2], 14 + pair)
                    return
                q = b
                inring = q in RINGED
                if q in loaded(p):
                    pe.wait_ge(split_ready, split_no(p, c, q) + 1)
                if isinstance(c, int) and c == 0 and q % 2 == 0:
                    if p == L3:
                        pe.wait_ge(nat_used, nat_no(L2, q // 2, 1) + 1)
                    else:
                        pe.wait_ge(x_ready, q // 4 + 1 if p == L0 else PRO_GROUPS + x_no(p - 1, q // 2) + 1)
                for k in range(TQ):
                    t = TQ * q + k
                    first, end = t == 0, t == NT - 1
                    if inring:
                        hi, lo = (ringed(RINGED.index(q), part, k, 1) for part in range(2))
                    else:
                        hi, lo = (cached(c, q, part, k, 1) for part in range(2))
                    acc = accA[:, par, :]
                    both = tile(x, t, 2, 2 * D)
                    nc.tensor.matmul(acc, both, hi, start=first, stop=end and p == L0)
                    if p == L0:
                        accb = spare[0:D + 2, par, :]
                        nc.tensor.matmul(accb, tile(x, t, 0, D + 2), lo, start=first, stop=False)
                        last = nc.tensor.matmul(accb, ones16[:, :], hi, start=False, stop=end)
                    else:
                        last = nc.tensor.matmul(acc, both, lo, start=False, stop=end)
                if inring:
                    last.then_inc(ring_done, 1)

            def triangle(c, pair):
                pe.wait_ge(u_ready, NT * c + 2 * pair + 2)
                if pair >= 2 or not (isinstance(c, int) and c == 0):
                    pe.wait_ge(w_ready, 16 * c + pair - 1)
                for i in range(2):
                    t = 2 * pair + i
                    o = spare[:, 2 * (pair % 2) + i, :]
                    last = nc.tensor.matmul(o, triA[:, :], uS[:, (t % 8) * W:(t % 8 + 1) * W],
                                            start=True, stop=(t == 0))
                    if t:
                        last = nc.tensor.matmul(o, triB[:, :], uS[:, ((t - 1) % 8) * W:((t - 1) % 8 + 1) * W],
                                                start=False, stop=True)
                last.then_inc(tri_done, 1)

            def weigh(c, par, pair):
                pe.wait_ge(w_ready, 16 * c + pair + 1)
                for i in range(2):
                    t = 2 * pair + i
                    w = wS[:, ((pair % 4) * 2 + i) * W:((pair % 4) * 2 + i + 1) * W].bitcast(BF16)
                    last = nc.tensor.matmul(accA[:, par, :], tile(X[L2 % 2], NT - 1 - t, 2, 2 * D), w,
                                            start=(t == 0), stop=(t == NT - 1))
                last.then_inc(w_used, 1)

            def step(p, c, par, before):
                early = p == L2 and isinstance(c, int) and c == 0
                if early:
                    for at in range(8):
                        epilogue(at, before)
                    pe.wait_ge(nat_used, nat_no(L1B, NC - 1, 1) + 1)
                s = NC * p + c
                if not (isinstance(c, int) and c < 2 and p == L0):
                    pe.wait_ge(acc_evac, s - 1)
                    if p == L0:
                        pe.wait_ge(accb_evac, s - 1)
                if p == L3 and isinstance(c, int) and c == 0:
                    for pair in (14, 15):
                        weigh(before[1], before[2], pair)
                for b in range(NQ):
                    main(p, c, par, b, before)
                    if b % 2 and before and not early:
                        epilogue(b // 2, before)

            def finish(before):
                for at in range(8):
                    epilogue(at, before)

            pe.wait_ge(const_ready, 1)
            sweep_steps(pe, step, finish)


def kernel(x, adj, L0_gnn_t, L1_gnn_W, L2_gnn_weight, L2_gnn_bias, L3_gnn_t, L3_gnn_B, L3_gnn_W1,
           L3_gnn_b1, L3_gnn_W2, L3_gnn_b2):
    import concourse.bacc as bacc
    from concourse.bass_utils import run_bass_kernel_spmd

    def host(a):
        return np.asarray(a)

    x_rows = np.ascontiguousarray(host(x).reshape(NT, P, D).transpose(1, 0, 2)).reshape(P, NT * D)
    blocks = np.ascontiguousarray(host(adj).reshape(NC, W, NQ, TQ, P).transpose(0, 2, 4, 3, 1))
    blocks = blocks.reshape(NC * NQ * P, BLK)

    wts = np.zeros((P, NCOLS), np.float32)

    def put(name, a):
        lo, hi = COLS[name]
        wts[0:a.shape[0], lo:hi] = a

    for k in range(2):
        for h in range(2):
            lo, hi = COLS[f"wagg{k}"]
            wts[h * D:(h + 1) * D, lo:hi] = host(L1_gnn_W)[k, 0:D]
            lo, hi = COLS[f"wx{k}"]
            wts[h * D:(h + 1) * D, lo:hi] = host(L1_gnn_W)[k, D:2 * D]
    put("l2w", host(L2_gnn_weight))
    put("bT", host(L3_gnn_B).T)
    put("w1", host(L3_gnn_W1)[0:D])
    put("w2", host(L3_gnn_W2).reshape(2, P, D).transpose(1, 0, 2).reshape(P, 2 * D))
    put("w1t", host(L3_gnn_W1)[D].reshape(2, P).T)
    put("b1", host(L3_gnn_b1).reshape(2, P).T)
    put("t", np.broadcast_to(host(L3_gnn_t).reshape(1, 1), (P, 1)))
    put("bias", np.broadcast_to(host(L2_gnn_bias).reshape(1, D), (P, D)))
    put("b2", np.broadcast_to(host(L3_gnn_b2).reshape(1, D), (P, D)))
    put("ident", np.eye(P, dtype=np.float32))
    eye = np.eye(D, dtype=np.float32)
    put("joinA", np.concatenate([np.concatenate([eye, eye], 0), np.zeros((P, 1), np.float32)], 1))
    join_b = np.zeros((P, D + 1), np.float32)
    join_b[2:2 + D, 0:D] = eye
    join_b[0, D] = 1.0
    put("joinB", join_b)
    i, j = np.arange(P)[:, None], np.arange(P)[None, :]
    tri_a = np.where(i > j, -BIT, np.where(i == j, NEIGH * BIT, 0.0)).astype(np.float32)
    tri_b = np.float32(-BIT) - tri_a
    tri = np.concatenate([tri_a, tri_b], 1)

    nc = bacc.Bacc("TRN2", target_bir_lowering=False, num_devices=1)
    arrays = {"x_rows": x_rows, "adj_blocks": blocks, "weights": wts, "triangles": tri}
    args = [nc.dram_tensor(n, a.shape, mybir.dt.from_np(a.dtype), kind="ExternalInput").ap()
            for n, a in arrays.items()]
    out = nc.dram_tensor("out_rows", (P, NT * D), F32, kind="ExternalOutput").ap()
    gnn_kernel(nc, *args, out)
    r = run_bass_kernel_spmd(nc, [arrays], core_ids=[0])
    got = r.results[0]["out_rows"]
    return np.ascontiguousarray(got.reshape(P, NT, D).transpose(1, 0, 2)).reshape(N, D)
```

```python
from contextlib import ExitStack

import numpy as np

import concourse.bass as bass
from concourse import mybir

ALU = mybir.AluOpType
ACT = mybir.ActivationFunctionType
AX_X = mybir.AxisListType.X
F32 = mybir.dt.float32
F16 = mybir.dt.float16
BF16 = mybir.dt.bfloat16
U16 = mybir.dt.uint16

P = 128
N = 4096
D = 64
NT = N // P
W = 512
NC = N // W
TQ = 2
NQ = NT // TQ
BLK = TQ * W
EPS = 1e-5
PRO_GROUPS = 4

PRO_ACT = {3: (("square", 1),), 5: (("rows", 1), ("square", 2)), 9: (("rows", 2), ("square", 3)), 13: (("rows", 3),)}
PRO_DVE = {0: (("variance", 1),), 2: (("scale", 1),), 4: (("variance", 2),), 6: (("scale", 2),),
           8: (("variance", 3),), 10: (("scale", 3),)}

L0, L1A, L1B, L2, L3 = range(5)
SPLIT_SWEEPS = (L0, L1A, L1B, L3)
CACHED = tuple(range(0, NQ, 4))
RINGED = tuple(q for q in range(NQ) if q % 4)
NR = len(RINGED)
LAND = 8
SLOTS = (1, 2, 3, 5, 6, 7)
RING = 4

SCALE = 4096.0
ROOT = SCALE * float(np.sqrt(D))
UNSCALE = 1.0 / (SCALE * SCALE)
NEIGH = 100
BIT = 128.0
L2_UNSCALE = 2.0 ** (127 - NEIGH) / SCALE
XW = 2 * D + 2

COLS = {}
_at = 0
for _name, _n in (("wagg0", D), ("wx0", D), ("wagg1", D), ("wx1", D), ("l2w", D), ("bT", D), ("w1", 256),
                  ("w2", 2 * D), ("w1t", 2), ("b1", 2), ("t", 1), ("bias", D), ("b2", D),
                  ("ident", P), ("joinA", D + 1), ("joinB", D + 1)):
    COLS[_name] = (_at, _at + _n)
    _at += _n
NCOLS = _at
LN_STEPS = 2
EPI_LINKS = {L0: 4 + LN_STEPS, L1A: 0, L1B: LN_STEPS, L2: LN_STEPS, L3: LN_STEPS}


def loaded(p):
    if p == L0:
        return list(range(NQ))
    return list(reversed(RINGED)) if p == L2 else list(RINGED)


def slot(p, q):
    return q % LAND if p == L0 else SLOTS[loaded(p).index(q) % len(SLOTS)]


def landed_no(p, c, q):
    second = loaded(p).index(q) >= (LAND if p == L0 else len(SLOTS))
    return (2 * (NC * p + c) + (1 if second else 0) + 1) * 16


def split_no(p, c, q):
    if p == L0:
        return NQ * c + q
    before = {L1A: 0, L1B: 1, L3: 2}[p]
    return NQ * NC + NR * NC * before + NR * c + RINGED.index(q)


def ring_no(p, c, q):
    return NR * (NC * SPLIT_SWEEPS.index(p) + c) + RINGED.index(q)


def nat_no(p, c, i=0):
    return {L0: c, L1A: 8 + c, L1B: 16 + 2 * c + i, L2: 32 + 2 * c + i, L3: 48 + c}[p]


def tr_no(p, c, i=0):
    return {L1A: c, L1B: 8 + 2 * c + i, L2: 24 + c, L3: 32 + c}[p]


def row_no(p, c):
    return {L0: c, L1B: 8 + c, L2: 16 + c, L3: 24 + c}[p]


def ready_no(p, c):
    return {L0: 0, L2: NC}[p] + c


def h_no(p, c):
    return {L0: 0, L1B: NC, L2: 2 * NC, L3: 3 * NC}[p] + c


def x_no(p, c):
    return NC * p + c


def norm_no(p, c):
    return PRO_GROUPS + {L0: 0, L1B: NC, L2: 2 * NC, L3: 3 * NC}[p] + c


def ln_no(p, c):
    return norm_no(p, c) - PRO_GROUPS


def link_base(p, c):
    return PROLOGUE_LINKS + sum(NC * EPI_LINKS[k] for k in range(p)) + EPI_LINKS[p] * c


PROLOGUE_LINKS = 7 + 1 + (PRO_GROUPS - 1)


STAGES = 8
HELD = 2
LATE = (8,)
HT_PE = {L1B: 5, L2: 6}
HT_ACT = {L1B: 6, L2: 7}
ROW_STAGES = {"rows": 0, "centre": 2, "variance": 3, "norm": 5, "transpose": 5, "transposed": 9, "hidden": 9,
              "tanh0": 13, "tanh1": 14, "intra": 15}
ROW_STAGES_00 = {"rows": 9, "centre": 12, "variance": 14}
ROW_STAGES_0 = {"norm": 0, "transpose": 0, "transposed": 4, "hidden": 4, "tanh0": 7, "tanh1": 8, "intra": 9}
ROW_STAGES_1 = {"rows": 2, "centre": 5, "variance": 6, "norm": 8, "transpose": 8, "transposed": 11, "hidden": 11,
                "tanh0": 14, "tanh1": 15, "intra": 15}
STAGES_L1B = {0: 1, 1: 3, 3: 7, 4: 8, 5: 10, 6: 14, 7: 15}
QUICK = {L1A: {0: 0, 1: 1, 3: 4, 4: 5, 5: 6, 6: 7, 7: 9}, L1B: {0: 0, 1: 1, 3: 4},
         L2: {3: 2, 4: 3, 5: 5, 6: 7, 7: 8, 8: 8},
         L3: {0: 1, 1: 1, 2: 3, 4: 3, 5: 5, 6: 6, 7: 10, 8: 12}}
SUM_STAGES = {"sums": 3, "summed": 7, "add": 10, "result": 11, "store": 13}


def stages_after(p, c, par, b, before, before2):
    def at_block(stages, e):
        return [(k, e) for k, at in stages.items() if at == b]

    if p != L0 and isinstance(c, int) and c == 0:
        found = at_block(QUICK[p], before)
        return found + at_block(ROW_STAGES_00, (p, c, par)) if p == L3 else found
    if p == L3:
        found = at_block(SUM_STAGES, before)
        if isinstance(c, int) and c == 1:
            return found + at_block(ROW_STAGES_0, before) + at_block(ROW_STAGES_1, (p, c, par))
        return found + at_block(ROW_STAGES, (p, c, par))
    if p == L1B:
        return at_block({8: 2}, before2) if before2 and b == 2 else at_block(STAGES_L1B, before)
    found = []
    if b % 2 and before:
        if before2 and p == L2 and STAGES + b // 2 in LATE:
            found.append((STAGES + b // 2, before2))
        found.append((b // 2, before))
    return found


def early_stages(p, c, before, before2):
    if p == L3 and isinstance(c, int) and c == 0:
        return [(k, before2) for k in LATE]
    if p == L2 and isinstance(c, int) and c == 0:
        return [(8, before2), (0, before), (1, before)]
    return []


def last_stages(before, before2):
    return [(k, before) for k in SUM_STAGES]


def sweep_steps(eng, step, finish):
    for p in range(5):
        step(p, 0, 0, (p - 1, NC - 1, 1) if p else None, (p - 1, NC - 2, 0) if p else None)
        step(p, 1, 1, (p, 0, 0), None)
        with eng.Fori(2, NC - 1, 2) as c:
            step(p, c, 0, (p, c - 1, 1), (p, c - 2, 0))
            step(p, c + 1, 1, (p, c, 0), (p, c - 1, 1))
    finish((L3, NC - 1, 1), (L3, NC - 2, 0))


def gnn_kernel(nc, x_in, adj_in, wts_in, tri_in, out):
    x1_d = nc.dram_tensor("x1_rows", (P, NT * D), F32, kind="Internal").ap()
    x2_d = nc.dram_tensor("x2_rows", (P, NT * D), F32, kind="Internal").ap()
    x3_d = nc.dram_tensor("x3_rows", (P, NT * D), F32, kind="Internal").ap()
    rows_from = {L0: x_in, L1B: x1_d, L2: x2_d, L3: x3_d}
    rows_to = {L0: x1_d, L1B: x2_d, L2: x3_d, L3: out}

    with ExitStack() as ctx:
        def sb(name, shape, dt):
            return ctx.enter_context(nc.sbuf_tensor(name, shape, dt))

        def psum(name, shape, dt):
            return ctx.enter_context(nc.psum_tensor(name, shape, dt))

        def sem(name):
            return ctx.enter_context(nc.semaphore(name))

        cache = sb("cache", [P, NC * len(CACHED) * 2 * BLK], F16)
        ring = sb("ring", [P, RING, 2 * BLK], F16)
        land = sb("land", [P, LAND, BLK], F32)
        X = [sb(f"X{i}", [P, NT * XW], F16) for i in range(2)]
        wts = sb("wts", [P, NCOLS], F32)
        ident16 = sb("ident16", [P, P], F16)
        ones16 = sb("ones16", [P, D + 2], F16)
        triA = sb("triA", [P, P], BF16)
        triB = sb("triB", [P, P], BF16)
        accS = sb("accS", [P, W], F32)
        accBS = sb("accBS", [P, W], F32)
        natS = sb("natS", [P, 4 * (D + 1)], F32)
        xin = sb("xin", [P, 4 * D], F32)
        zS = sb("zS", [P, 4 * D], F32)
        tS = sb("tS", [P, 4 * D], F32)
        hS = sb("hS", [P, 4 * D], F32)
        rowsum = sb("rowsum", [P, NT], F32)
        st = sb("st", [P, 16], F32)
        var = sb("var", [P, 8], F32)
        rstd = sb("rstd", [P, 8], F32)
        power = sb("power", [P, 8], F32)
        scale = sb("scale", [P, 1], F32)
        hbias = sb("hbias", [P, 2], F32)
        uS = ring[:, 0:2, :].rearrange("p a n -> p (a n)").bitcast(BF16)
        wS = ring[:, 2:4, :].rearrange("p a n -> p (a n)")
        hidS = land[:, 0, :]
        mS = land[:, 0, :].bitcast(BF16)
        heldS = land[:, 4, :].bitcast(BF16)
        yS = land[:, 4, 0:4 * D]
        sideS = land[:, 4, :]
        x_all = cache[:, 15 * NT * P:16 * NT * P].bitcast(F32)
        pro = cache[:, 14 * NT * P:15 * NT * P].bitcast(F32)
        tri_f = cache[:, 13 * NT * P:14 * NT * P].bitcast(F32)
        pro_sq = cache[:, 12 * NT * P:13 * NT * P].bitcast(F32)
        pro_h = cache[:, 11 * NT * P:12 * NT * P].bitcast(F32)
        pro_stats = tri_f[:, 2 * P:2 * P + 4 * NT]

        def pro_stat(k, g, n=1):
            return pro_stats[:, k * NT + g * 8:k * NT + (g + n) * 8]

        def pro_group(t, g, n=1):
            return t[:, g * 8 * D:(g + n) * 8 * D]


        accA = psum("accA", [P, 2, W], F32)
        spare = psum("spare", [P, 4, W], F32)
        intra_p, hidden_p = spare[:, 0, 0:4 * D], spare[:, 2:4, :]
        nat = psum("nat", [P, W], F32)
        tr = psum("tr", [P, W], F32)

        landed = [sem(f"landed{i}") for i in range(LAND)]
        wts_in_s, tri_in_s, x_in_s = sem("wts_in"), sem("tri_in"), sem("x_in")
        hi_ready = sem("hi_ready")
        split_ready = sem("split_ready")
        ring_done = sem("ring_done")
        acc_evac, accb_evac = sem("acc_evac"), sem("accb_evac")
        nat_done, nat_evac, nat_used = sem("nat_done"), sem("nat_evac"), sem("nat_used")
        tr_done, tr_evac = sem("tr_done"), sem("tr_evac")
        h_ready = sem("h_ready")
        x_ready = sem("x_ready")
        hi_rows = sem("hi_rows")
        link = sem("link")
        const_ready = sem("const_ready")
        rows_in, rows_out = sem("rows_in"), sem("rows_out")
        rows_used, rows_ready = sem("rows_used"), sem("rows_ready")
        var_ready, rstd_ready = sem("var_ready"), sem("rstd_ready")
        mean_ready, centred = sem("mean_ready"), sem("centred")
        squared, scaled = sem("squared"), sem("scaled")
        pro_rows = sem("pro_rows")
        power_ready = sem("power_ready")
        u_ready = sem("u_ready")
        mask_ready = sem("mask_ready")
        tri_done = sem("tri_done")
        w_ready = sem("w_ready")
        w_used = sem("w_used")
        rows_centred, rows_squared, rows_scaled = sem("rows_centred"), sem("rows_squared"), sem("rows_scaled")
        side_step = sem("side_step")
        side_ready = sem("side_ready")
        hidden_done, hidden_ready = sem("hidden_done"), sem("hidden_ready")
        intra_done, intra_used = sem("intra_done"), sem("intra_used")

        def wt(name, rows=P, lo=0, hi=None):
            a, b = COLS[name]
            return wts[0:rows, a + lo:(b if hi is None else a + hi)]

        def chunk_tiles(x, c, lo, n):
            v = x[:, bass.ds(c * (4 * XW), 4 * XW)].rearrange("p (t w) -> p t w", w=XW)
            return v[:, :, lo:lo + n]

        def tile(x, t, lo, n):
            return x[:, t * XW + lo:t * XW + lo + n]

        def cached(c, q, part, k=0, n=TQ):
            return cache[:, bass.ds(c * (len(CACHED) * 2 * BLK) + ((q // 4) * 2 + part) * BLK + k * W, n * W)]

        def ringed(r, part, k=0, n=TQ):
            return ring[:, r % RING, part * BLK + k * W:part * BLK + (k + n) * W]

        def weights(c, pair):
            if isinstance(c, int) and c == 0 and pair < HELD:
                return heldS[:, pair * 2 * W:(pair + 1) * 2 * W]
            return wS[:, (pair % 4) * 2 * W:(pair % 4 + 1) * 2 * W]

        def rows4(t):
            return t[:, 0:4 * D].rearrange("p (t d) -> p t d", d=D)

        def spread(col):
            return col.rearrange("p (t o) -> p t o", o=1).to_broadcast([P, col.shape[1], D])

        def over_tiles(name):
            return wt(name).rearrange("p (o d) -> p o d", o=1).to_broadcast([P, 4, D])

        block = ctx.enter_context(nc.Block())

        @block.sync
        def _(sp):
            sp.dma_start(x_all, x_in).then_inc(x_in_s, 16)
            sp.dma_start(wts[:, :], wts_in).then_inc(wts_in_s, 16)
            sp.dma_start(tri_f[:, 0:2 * P], tri_in).then_inc(tri_in_s, 16)

            def step(p, c, par, before, before2):
                qs = loaded(p)
                for i, q in enumerate(qs):
                    if p == L0:
                        if i >= LAND:
                            sp.wait_ge(split_ready, split_no(p, c, q - LAND) + 1)
                        elif not (isinstance(c, int) and c == 0):
                            sp.wait_ge(split_ready, split_no(p, c - 1, q + LAND) + 1)
                    else:
                        if i >= len(SLOTS):
                            pp, pc, pq = p, c, qs[i - len(SLOTS)]
                        elif not (isinstance(c, int) and c == 0):
                            pp, pc, pq = p, c - 1, qs[i + len(SLOTS)]
                        else:
                            pp, pc = p - 1, NC - 1
                            pq = [b for b in loaded(pp) if slot(pp, b) == slot(p, q)][-1]
                        if pp == L2:
                            sp.wait_ge(mask_ready, (NT - 1) * (pc + 1) - TQ * pq)
                        else:
                            sp.wait_ge(split_ready, split_no(pp, pc, pq) + 1)
                    sp.dma_start(land[:, slot(p, q), :], adj_in[bass.ds(c * (NQ * P) + q * P, P), :])\
                        .then_inc(landed[slot(p, q)], 16)

            sweep_steps(sp, step, lambda before, before2: None)

        @block.gpsimd
        def _(pool):
            def inverse_root(number, ntile, out=rstd, of=var):
                pool.wait_ge(var_ready, number + 1)
                nc.gpsimd.tensor_tensor(out[:, 0:ntile], of[:, 0:ntile], power[:, 0:ntile], ALU.pow)\
                    .then_inc(rstd_ready, 1)

            def layernorm(p, c):
                m = ln_no(p, c)
                pool.wait_ge(rows_centred, m + 1)
                nc.gpsimd.tensor_tensor(hS[:, :], tS[:, :], tS[:, :], ALU.mult).then_inc(rows_squared, 1)
                inverse_root(norm_no(p, c), 4)
                pool.wait_ge(rstd_ready, norm_no(p, c) + 1)
                nc.gpsimd.tensor_tensor(rows4(tS), rows4(tS), spread(rstd[:, 0:4]), ALU.mult).then_inc(rows_scaled, 1)

            def side(c, par):
                out = sideS[:, par * 4 * D:(par + 1) * 4 * D]
                here = X[L3 % 2]
                if not (isinstance(c, int) and c < 2):
                    pool.wait_ge(nat_used, nat_no(L3, c - 1))
                pool.wait_ge(rows_in, (row_no(L3, c) + 1) * 16)
                nc.gpsimd.tensor_tensor(rows4(out), chunk_tiles(here, c, 2, D), chunk_tiles(here, c, 2 + D, D),
                                        ALU.add).then_inc(side_step, 1)
                pool.wait_ge(side_step, 3 * c + 1)
                nc.gpsimd.tensor_tensor(rows4(out), rows4(out), spread(rowsum[:, bass.ds(c * 4, 4)]), ALU.mult)\
                    .then_inc(side_step, 1)
                pool.wait_ge(side_step, 3 * c + 2)
                nc.gpsimd.tensor_tensor(out, out, xin[:, :], ALU.add).then_inc(side_step, 1)
                pool.wait_ge(side_step, 3 * c + 3)
                nc.gpsimd.tensor_tensor(rows4(out), rows4(out), over_tiles("b2"), ALU.add).then_inc(side_ready, 1)

            def split_rows(p, c):
                nxt = X[(p + 1) % 2]
                hi, lo = chunk_tiles(nxt, c, 2, D), chunk_tiles(nxt, c, 2 + D, D)
                if p == L0:
                    pool.wait_ge(h_ready, h_no(p, c) + 1)
                    v = rows4(hS)
                elif p == L1A:
                    pool.wait_ge(x_ready, PRO_GROUPS + x_no(p, c))
                    pool.wait_ge(nat_evac, nat_no(p, c, 0) + 1)
                    nc.gpsimd.tensor_tensor(yS[:, :], natS[:, 0:4 * D], scale[:, 0:1].to_broadcast([P, 4 * D]), ALU.mult)\
                        .then_inc(nat_used, 1)
                    pool.wait_ge(nat_used, nat_no(p, c, 0) + 1)
                    v = rows4(yS)
                else:
                    pool.wait_ge(nat_evac, nat_no(p, c, 1) + 1)
                    v = rows4(natS)
                nc.gpsimd.tensor_copy(hi, v).then_inc(hi_rows, 1)
                pool.wait_ge(hi_rows, x_no(p, c) + 1)
                nc.gpsimd.tensor_tensor(lo, v, hi, ALU.subtract)\
                    .then_inc(x_ready if p in (L0, L1A) else nat_used, 1)

            def epilogue(e):
                p, c, par = e
                if p != L1A:
                    layernorm(p, c)
                split_rows(p, c)

            def step(p, c, par, before, before2):
                if p == L3 and isinstance(c, int) and c == 1:
                    layernorm(p, 0)
                    side(0, 0)
                elif before and before[0] != L3:
                    epilogue(before)
                if p == L3 and not (isinstance(c, int) and c == 0):
                    layernorm(p, c)
                    side(c, par)

            nc.gpsimd.memset(power[:, :], -0.5).then_inc(power_ready, 1)
            nc.gpsimd.memset(scale[:, :], SCALE).then_inc(power_ready, 1)
            pool.wait_ge(power_ready, 2)
            inverse_root(0, 8)
            pool.wait_ge(mean_ready, 1)
            for g in range(1, PRO_GROUPS):
                z, t = (pro_group(a, g).rearrange("p (t d) -> p t d", d=D) for a in (x_all, pro))
                nc.gpsimd.tensor_tensor(t, z, spread(pro_stat(1, g)), ALU.add).then_inc(centred, 1)
            for g in range(1, PRO_GROUPS):
                inverse_root(g, 8, pro_stat(3, g), pro_stat(2, g))
                pool.wait_ge(pro_rows, 2 * g)
                v = X[0][:, g * 8 * XW:(g + 1) * 8 * XW].rearrange("p (t w) -> p t w", w=XW)
                nc.gpsimd.tensor_tensor(v[:, :, 2 + D:2 + 2 * D], pro_group(pro_h, g).rearrange("p (t d) -> p t d", d=D),
                                        v[:, :, 2:2 + D], ALU.subtract).then_inc(x_ready, 1)
            sweep_steps(pool, step, lambda before, before2: None)

        @block.scalar
        def _(act):
            def xin_read(p, c):
                if p == L0:
                    act.wait_ge(rows_used, c + 1)
                elif p == L3:
                    act.wait_ge(side_ready, c + 1)
                else:
                    act.wait_ge(nat_used, nat_no(p, c, 0) + 1)

            def epilogue(at, e):
                p, c, par = e
                if at == ("rows" if p == L3 else 0) and p in rows_from:
                    if not (isinstance(c, int) and c == 0):
                        xin_read(p, c - 1)
                    elif p != L0:
                        xin_read({L1B: L0, L2: L1B, L3: L2}[p], NC - 1)
                    act.dma_start(xin[:, :], rows_from[p][:, bass.ds(c * (4 * D), 4 * D)]).then_inc(rows_in, 16)
                if at == {L2: 0, L3: "sums"}.get(p, 1):
                    if p == L2:
                        act.wait_ge(w_used, 16 * (c + 1))
                    else:
                        act.wait_ge(ring_done, ring_no(p, c, NQ - 1) + 1)
                    if not (isinstance(c, int) and c == 0 and p == L0):
                        act.wait_ge(nat_done, nat_no(p, c, 0))
                    nc.scalar.activation(accS[:, :], accA[:, par, :], ACT.Copy,
                                         scale=L2_UNSCALE if p == L2 else UNSCALE).then_inc(acc_evac, 1)
                    if p == L0:
                        nc.scalar.activation(accBS[0:D + 2, :], spare[0:D + 2, par, :], ACT.Copy, scale=UNSCALE)\
                            .then_inc(accb_evac, 1)
                    if p in (L1A, L1B):
                        act.wait_ge(tr_done, tr_no(p, c, 0) + 1)
                        nc.scalar.activation(accBS[:, :], tr[:, 0:W // 2].bitcast(F16), ACT.Copy, scale=1.0 / SCALE)\
                            .then_inc(tr_evac, 1)
                if at == {L2: 2, L3: "summed"}.get(p, 3):
                    n = nat_no(p, c, 0)
                    act.wait_ge(nat_done, n + 1)
                    if not (isinstance(n, int) and n == 0):
                        act.wait_ge(nat_used, n)
                    width = 4 * (D + 1) if p == L0 else 4 * D
                    nc.scalar.activation(natS[:, 0:width], nat[:, 0:width],
                                         ACT.Tanh if p in (L1A, L1B) else ACT.Copy).then_inc(nat_evac, 1)
                if at == ("transposed" if p == L3 else HT_ACT.get(p, None)):
                    i = 1 if p == L1B else 0
                    act.wait_ge(tr_done, tr_no(p, c, i) + 1)
                    nc.scalar.activation(accBS[0:D, :], tr[0:D, :], ACT.Copy).then_inc(tr_evac, 1)
                if at == 8 and p in (L1B, L2):
                    n = nat_no(p, c, 1)
                    act.wait_ge(nat_done, n + 1)
                    act.wait_ge(nat_used, n)
                    nc.scalar.activation(natS[:, 0:4 * D], nat[:, 0:4 * D], ACT.Copy, scale=SCALE)\
                        .then_inc(nat_evac, 1)
                if p == L3 and at in ("tanh0", "tanh1"):
                    h = int(at[-1])
                    act.wait_ge(hidden_done, c + 1)
                    if h == 0 and not (isinstance(c, int) and c == 0):
                        act.wait_ge(intra_done, c)
                    nc.scalar.activation(hidS[:, h * W:(h + 1) * W], hidden_p[:, h, :], ACT.Tanh,
                                         bias=hbias[:, h:h + 1]).then_inc(hidden_ready, 1)
                if at == ("store" if p == L3 else 7) and p in rows_to:
                    if p in (L1B, L3):
                        act.wait_ge(nat_used, nat_no(p, c, 0) + 1)
                    else:
                        act.wait_ge(rows_ready, ready_no(p, c) + 1)
                    act.dma_start(rows_to[p][:, bass.ds(c * (4 * D), 4 * D)], zS[:, :]).then_inc(rows_out, 16)

            def main(p, c, par, b):
                if p == L2:
                    pair = b
                    act.wait_ge(tri_done, 16 * c + pair + 1)
                    if not (isinstance(c, int) and c == 0):
                        act.wait_ge(w_used, 16 * c + pair - 3)
                    elif pair >= HELD + 4:
                        act.wait_ge(w_used, pair - 3 - HELD)
                    k = pair % 2
                    nc.scalar.activation(weights(c, pair).bitcast(U16),
                                         spare[:, 2 * k:2 * k + 2, :].rearrange("p a b -> p (a b)"), ACT.Relu)\
                        .then_inc(w_ready, 1)
                    return
                q = b
                if q not in loaded(p):
                    return
                act.wait_ge(landed[slot(p, q)], landed_no(p, c, q))
                if p == L0 and q in CACHED:
                    hi = cached(c, q, 0)
                else:
                    n = ring_no(p, c, q)
                    if not (isinstance(n, int) and n < RING):
                        act.wait_ge(ring_done, n - RING + 1)
                    if p == L3 and isinstance(c, int) and c == 0 and q == RINGED[2]:
                        act.wait_ge(w_used, 16 * NC)
                    hi = ringed(RINGED.index(q), 0)
                nc.scalar.activation(hi, land[:, slot(p, q), :], ACT.Copy, scale=SCALE).then_inc(hi_ready, 1)

            def prologue(what, g):
                if what == "square":
                    act.wait_ge(centred, g)
                    nc.scalar.activation(pro_group(pro_sq, g), pro_group(pro, g), ACT.Square).then_inc(squared, 1)
                else:
                    act.wait_ge(scaled, g)
                    v = X[0][:, g * 8 * XW:(g + 1) * 8 * XW].rearrange("p (t w) -> p t w", w=XW)
                    t = pro_group(pro, g)
                    nc.scalar.activation(pro_group(pro_h, g), t, ACT.Relu, scale=ROOT).then_inc(pro_rows, 1)
                    nc.scalar.activation(v[:, :, 2:2 + D], t.rearrange("p (t d) -> p t d", d=D), ACT.Relu, scale=ROOT)\
                        .then_inc(pro_rows, 1)

            def step(p, c, par, before, before2):
                for k, e in early_stages(p, c, before, before2):
                    epilogue(k, e)
                for b in range(NQ):
                    main(p, c, par, b)
                    if p == L0 and isinstance(c, int) and c == 0:
                        for what, g in PRO_ACT.get(b, ()):
                            prologue(what, g)
                    for k, e in stages_after(p, c, par, b, before, before2):
                        epilogue(k, e)

            def finish(before, before2):
                for k, e in last_stages(before, before2):
                    epilogue(k, e)
                act.wait_ge(rows_out, 16 * 4 * NC)

            sweep_steps(act, step, finish)

        @block.vector
        def _(dve):
            class Links:
                def __init__(self, base):
                    self.base, self.n = base, 0

                def wait(self):
                    dve.wait_ge(link, self.base + self.n)

                def __call__(self, ins):
                    ins.then_inc(link, 1)
                    self.n += 1
                    self.wait()

            def centre(L, z, t, ntile):
                zv, tv = (a.rearrange("p (t d) -> p t d", d=D) for a in (z, t))
                L(nc.vector.tensor_reduce(st[:, 0:ntile], zv, AX_X, ALU.add))
                return nc.vector.scalar_tensor_tensor(out=tv, in0=spread(st[:, 0:ntile]), scalar=-1.0 / D, in1=zv,
                                                      op0=ALU.mult, op1=ALU.add)

            def variance(L, s0, ntile):
                L(nc.vector.tensor_reduce(st[:, 8:8 + ntile], s0.rearrange("p (t d) -> p t d", d=D), AX_X, ALU.add))
                nc.vector.tensor_scalar(var[:, 0:ntile], st[:, 8:8 + ntile], D * EPS, None, ALU.add)\
                    .then_inc(var_ready, 1)

            def centre_rows(L, z):
                centre(L, z, tS[:, :], 4).then_inc(rows_centred, 1)

            def variance_rows(L, p, c):
                dve.wait_ge(rows_squared, ln_no(p, c) + 1)
                variance(L, hS[:, :], 4)

            def norm_rows(p, c, scale):
                dve.wait_ge(rows_scaled, ln_no(p, c) + 1)
                nc.vector.tensor_scalar(hS[:, :], tS[:, :], 0.0, scale * float(np.sqrt(D)), ALU.max, ALU.mult)\
                    .then_inc(h_ready, 1)

            links = {}

            def epilogue(at, e):
                p, c, par = e
                if at in (0, "centre"):
                    links[0] = Links(link_base(p, c))
                L = links[0]
                n0 = nat_no(p, c, 0)
                if p == L1A:
                    return
                k = row_no(p, c)

                def sums_in():
                    dve.wait_ge(nat_evac, n0 + 1)

                def rows_in_sbuf():
                    dve.wait_ge(rows_in, (k + 1) * 16)

                def rows_written():
                    if not (isinstance(k, int) and k == 0):
                        dve.wait_ge(rows_out, k * 16)

                if p == L0:
                    n5 = natS[:, 0:4 * (D + 1)].rearrange("p (t d) -> p t d", d=D + 1)
                    here = X[L0 % 2]
                    if at == 3:
                        sums_in()
                        if not (isinstance(c, int) and c == 0):
                            dve.wait_ge(x_ready, PRO_GROUPS + c)
                        L(nc.vector.tensor_tensor(rows4(hS), chunk_tiles(here, c, 2, D),
                                                  chunk_tiles(here, c, 2 + D, D), ALU.add))
                        L(nc.vector.tensor_tensor(rows4(tS), rows4(hS), n5[:, :, 0:D], ALU.mult))
                        L(nc.vector.tensor_reduce(st[:, 0:4], rows4(tS), AX_X, ALU.add))
                        nc.vector.tensor_scalar(rowsum[:, bass.ds(c * 4, 4)].rearrange("p (t o) -> p t o", o=1),
                                                n5[:, :, D:D + 1], -1.0 / SCALE, None, ALU.mult).then_inc(nat_used, 1)
                    if at == 4:
                        L(nc.vector.tensor_scalar(st[:, 8:12], st[:, 0:4], -0.01 / SCALE, 1.0, ALU.mult, ALU.add))
                        rows_in_sbuf()
                        rows_written()
                        nc.vector.scalar_tensor_tensor(out=tS[:, :], in0=hS[:, :], scalar=-0.1 / SCALE,
                                                       in1=xin[:, :], op0=ALU.mult, op1=ALU.add).then_inc(rows_used, 1)
                        dve.wait_ge(rows_used, k + 1)
                        nc.vector.tensor_tensor(rows4(zS), rows4(tS), spread(st[:, 8:12]), ALU.add)\
                            .then_inc(rows_ready, 1)
                    if at == 5:
                        dve.wait_ge(rows_ready, ready_no(p, c) + 1)
                        centre_rows(L, zS[:, :])
                    if at == 6:
                        variance_rows(L, p, c)
                    if at == 7:
                        norm_rows(p, c, SCALE)
                elif p in (L1B, L2):
                    at = at - 1 if p == L2 else at
                    if at == 3:
                        sums_in()
                        rows_in_sbuf()
                        rows_written()
                        new = zS if p == L1B else tS
                        nc.vector.tensor_tensor(new[:, :], xin[:, :], natS[:, 0:4 * D], ALU.add).then_inc(nat_used, 1)
                        dve.wait_ge(nat_used, n0 + 1)
                        if p == L2:
                            nc.vector.tensor_tensor(rows4(zS), rows4(tS), over_tiles("bias"), ALU.add)\
                                .then_inc(rows_ready, 1)
                            dve.wait_ge(rows_ready, ready_no(p, c) + 1)
                        centre_rows(L, zS[:, :])
                    if at == 4:
                        variance_rows(L, p, c)
                    if at == 5:
                        norm_rows(p, c, 1.0)
                else:
                    side = sideS[:, par * 4 * D:(par + 1) * 4 * D]
                    if at == "centre":
                        rows_in_sbuf()
                        dve.wait_ge(tr_evac, tr_no(p, c, 0))
                        centre_rows(L, xin[:, :])
                    if at == "variance":
                        variance_rows(L, p, c)
                    if at == "norm":
                        norm_rows(p, c, 1.0)
                    if at == "add":
                        dve.wait_ge(intra_done, c + 1)
                        dve.wait_ge(side_ready, c + 1)
                        nc.vector.tensor_tensor(side, side, intra_p, ALU.add).then_inc(intra_used, 1)
                    if at == "result":
                        sums_in()
                        rows_written()
                        dve.wait_ge(intra_used, c + 1)
                        nc.vector.tensor_tensor(zS[:, :], side, natS[:, 0:4 * D], ALU.add).then_inc(nat_used, 1)

            def mask(c, b, halves):
                q = NQ - 1 - b
                for i in halves:
                    if q not in CACHED and i == 0:
                        dve.wait_ge(landed[slot(L2, q)], landed_no(L2, c, q))
                    if b == 0 and i == 0:
                        if isinstance(c, int) and c == 0:
                            dve.wait_ge(ring_done, ring_no(L1B, NC - 1, RINGED[-3]) + 1)
                        else:
                            dve.wait_ge(tri_done, 16 * c - 3)
                    k = TQ - 1 - i
                    src = cached(c, q, 0, k, 1) if q in CACHED else land[:, slot(L2, q), k * W:(k + 1) * W]
                    out = uS[:, 0:W] if b == 0 and i == 0 else mS[:, (b % 2) * BLK + i * W:(b % 2) * BLK + (i + 1) * W]
                    nc.vector.tensor_scalar(out, src, 0.0, None, ALU.not_equal)\
                        .then_inc(u_ready if b == 0 and i == 0 else mask_ready, 1)

            def main(p, c, par, b):
                if p == L2:
                    if b == 0:
                        mask(c, 0, (0, 1))
                    for i in range(TQ):
                        t = TQ * b + i
                        if t:
                            dve.wait_ge(mask_ready, (NT - 1) * c + t)
                            u = uS[:, (t % 8) * W:(t % 8 + 1) * W]
                            prev = uS[:, ((t - 1) % 8) * W:((t - 1) % 8 + 1) * W]
                            if t >= 8 or not (isinstance(c, int) and c == 0):
                                dve.wait_ge(tri_done, 16 * c + (t - 7) // 2 + 1)
                            dve.wait_ge(u_ready, NT * c + t)
                            nc.vector.tensor_tensor(u, mS[:, (b % 2) * BLK + i * W:(b % 2) * BLK + (i + 1) * W], prev,
                                                    ALU.add).then_inc(u_ready, 1)
                        if b < NQ - 1:
                            mask(c, b + 1, (i,))
                    return
                q = b
                if q not in loaded(p):
                    return
                n = split_no(p, c, q)
                dve.wait_ge(hi_ready, n + 1)
                if p == L0 and q in CACHED:
                    hi, lo = cached(c, q, 0), cached(c, q, 1)
                else:
                    hi, lo = ringed(RINGED.index(q), 0), ringed(RINGED.index(q), 1)
                nc.vector.scalar_tensor_tensor(out=lo, in0=land[:, slot(p, q), :], scalar=SCALE, in1=hi,
                                               op0=ALU.mult, op1=ALU.subtract).then_inc(split_ready, 1)

            def step(p, c, par, before, before2):
                first = p == L0 and isinstance(c, int) and c == 0
                for k, e in early_stages(p, c, before, before2):
                    epilogue(k, e)
                for b in range(NQ):
                    main(p, c, par, b)
                    if first:
                        for what, g in PRO_DVE.get(b, ()):
                            prologue(what, g)
                    for k, e in stages_after(p, c, par, b, before, before2):
                        epilogue(k, e)

            def finish(before, before2):
                for k, e in last_stages(before, before2):
                    epilogue(k, e)

            L = Links(0)
            h, t, s0 = pro_group(pro_h, 0), pro_group(pro, 0), pro_group(pro_sq, 0)
            dve.wait_ge(x_in_s, 16)
            L(centre(L, pro_group(x_all, 0), t, 8))
            L(nc.vector.tensor_tensor(s0, t, t, ALU.mult))
            variance(L, s0, 8)

            L(nc.vector.tensor_reduce(pro_stat(0, 1, PRO_GROUPS - 1),
                                      pro_group(x_all, 1, PRO_GROUPS - 1).rearrange("p (t d) -> p t d", d=D), AX_X,
                                      ALU.add))
            nc.vector.tensor_scalar(pro_stat(1, 1, PRO_GROUPS - 1), pro_stat(0, 1, PRO_GROUPS - 1), -1.0 / D, None,
                                    ALU.mult).then_inc(mean_ready, 1)
            xv = X[0][:, :].rearrange("p (t w) -> p t w", w=XW)
            nc.vector.memset(xv[:, :, 0:2], SCALE)
            nc.vector.memset(ones16[:, 2:D + 2], 0.0)
            nc.vector.memset(ones16[:, 0:2], SCALE)

            dve.wait_ge(rstd_ready, 1)
            tv = t.rearrange("p (t d) -> p t d", d=D)
            L(nc.vector.tensor_tensor(tv, tv, spread(rstd[:, 0:8]), ALU.mult))
            L(nc.vector.tensor_scalar(h, t, 0.0, ROOT, ALU.max, ALU.mult))
            hv = h.rearrange("p (t d) -> p t d", d=D)
            L(nc.vector.tensor_copy(xv[:, 0:8, 2:2 + D], hv))
            nc.vector.tensor_tensor(xv[:, 0:8, 2 + D:2 + 2 * D], hv, xv[:, 0:8, 2:2 + D], ALU.subtract)\
                .then_inc(x_ready, 1)

            def prologue(what, g):
                t, q = (pro_group(a, g).rearrange("p (t d) -> p t d", d=D) for a in (pro, pro_sq))
                if what == "variance":
                    dve.wait_ge(squared, g)
                    L(nc.vector.tensor_reduce(pro_stat(0, g), q, AX_X, ALU.add))
                    nc.vector.tensor_scalar(pro_stat(2, g), pro_stat(0, g), D * EPS, None, ALU.add)\
                        .then_inc(var_ready, 1)
                else:
                    dve.wait_ge(rstd_ready, g + 1)
                    nc.vector.tensor_tensor(t, t, spread(pro_stat(3, g)), ALU.mult).then_inc(scaled, 1)

            dve.wait_ge(wts_in_s, 16)
            dve.wait_ge(tri_in_s, 16)
            nc.vector.tensor_copy(ident16[:, :], wt("ident"))
            nc.vector.tensor_copy(triA[:, :], tri_f[:, 0:P])
            nc.vector.tensor_copy(triB[:, :], tri_f[:, P:2 * P])
            nc.vector.scalar_tensor_tensor(out=hbias[:, :], in0=wt("w1t"), scalar=wt("t"), in1=wt("b1"),
                                           op0=ALU.mult, op1=ALU.add).then_inc(const_ready, 1)
            sweep_steps(dve, step, finish)

        @block.tensor
        def _(pe):
            def nat_free(n):
                if not (isinstance(n, int) and n == 0):
                    pe.wait_ge(nat_evac, n)

            def tr_free(n):
                if not (isinstance(n, int) and n == 0):
                    pe.wait_ge(tr_evac, n)

            def acc_ordinal(p, c):
                return NC * p + c

            def epilogue(at, e):
                p, c, par = e
                if at == 0 and p in (L1A, L1B):
                    n = tr_no(p, c, 0)
                    tr_free(n)
                    x = X[p % 2]
                    for j in range(4):
                        last = nc.tensor.transpose(tr[:, j * D:(j + 1) * D].bitcast(F16),
                                                   x[:, bass.ds(c * (4 * XW) + j * XW + 2, 2 * D)], ident16[:, :])
                    last.then_inc(tr_done, 1)
                if at == ("sums" if p == L3 else 1):
                    n = nat_no(p, c, 0)
                    nat_free(n)
                    pe.wait_ge(acc_evac, acc_ordinal(p, c) + 1)
                    if p == L0:
                        pe.wait_ge(accb_evac, c + 1)
                        for j in range(4):
                            o = nat[:, j * (D + 1):(j + 1) * (D + 1)]
                            nc.tensor.matmul(o, accS[:, j * P:(j + 1) * P], wt("joinA"), start=True, stop=False)
                            last = nc.tensor.matmul(o, accBS[0:D + 2, j * P:(j + 1) * P], wt("joinB", D + 2),
                                                    start=False, stop=True)
                    elif p in (L1A, L1B):
                        pe.wait_ge(tr_evac, tr_no(p, c, 0) + 1)
                        k = 0 if p == L1A else 1
                        for j in range(4):
                            o = nat[:, j * D:(j + 1) * D]
                            nc.tensor.matmul(o, accS[:, j * P:(j + 1) * P], wt(f"wagg{k}"), start=True, stop=False)
                            last = nc.tensor.matmul(o, accBS[:, j * P:(j + 1) * P], wt(f"wx{k}"),
                                                    start=False, stop=True)
                    else:
                        for j in range(4):
                            last = nc.tensor.matmul(nat[:, j * D:(j + 1) * D], accS[:, j * P:(j + 1) * P],
                                                    wt("joinA", P, 0, D), start=True, stop=True)
                    last.then_inc(nat_done, 1)
                if at == ("transpose" if p == L3 else HT_PE.get(p, None)):
                    n = tr_no(p, c, 1 if p == L1B else 0)
                    tr_free(n)
                    pe.wait_ge(h_ready, h_no(p, c) + 1)
                    for j in range(4):
                        last = nc.tensor.matmul(tr[0:D, j * P:(j + 1) * P], hS[:, j * D:(j + 1) * D], wt("ident"),
                                                start=True, stop=True)
                    last.then_inc(tr_done, 1)
                if at == {L1B: 6, L2: 8}.get(p):
                    n = nat_no(p, c, 1)
                    nat_free(n)
                    pe.wait_ge(tr_evac, tr_no(p, c, 1 if p == L1B else 0) + 1)
                    w = wt("l2w" if p == L1B else "bT", D)
                    for j in range(4):
                        last = nc.tensor.matmul(nat[:, j * D:(j + 1) * D], accBS[0:D, j * P:(j + 1) * P], w,
                                                start=True, stop=True)
                    last.then_inc(nat_done, 1)
                if at == "hidden":
                    pe.wait_ge(tr_evac, tr_no(p, c, 0) + 1)
                    if not (isinstance(c, int) and c == 0):
                        pe.wait_ge(hidden_ready, 2 * c)
                    for h in range(2):
                        last = nc.tensor.matmul(hidden_p[:, h, :], wt("w1", D, h * P, (h + 1) * P), accBS[0:D, :],
                                                start=True, stop=True)
                    last.then_inc(hidden_done, 1)
                if at == "intra":
                    pe.wait_ge(hidden_ready, 2 * c + 2)
                    if not (isinstance(c, int) and c == 0):
                        pe.wait_ge(intra_used, c)
                    for j in range(4):
                        for h in range(2):
                            last = nc.tensor.matmul(intra_p[:, j * D:(j + 1) * D],
                                                    hidS[:, h * W + j * P:h * W + (j + 1) * P],
                                                    wt("w2", P, h * D, (h + 1) * D), start=(h == 0), stop=(h == 1))
                    last.then_inc(intra_done, 1)

            def main(p, c, par, b, before):
                x = X[p % 2]
                if p == L2:
                    pair = b
                    triangle(c, pair)
                    if isinstance(c, int) and c == 0:
                        if pair == HELD + 2:
                            pe.wait_ge(nat_used, nat_no(L1B, NC - 2, 1) + 1)
                        if pair >= HELD + 2:
                            weigh(c, par, pair - 2)
                        if pair == 15:
                            pe.wait_ge(nat_used, nat_no(L1B, NC - 1, 1) + 1)
                            for held in range(HELD):
                                weigh(c, par, held)
                    elif pair >= 2:
                        weigh(c, par, pair - 2)
                    elif before[0] == L2:
                        weigh(before[1], before[2], 14 + pair)
                    return
                q = b
                inring = q in RINGED
                if q in loaded(p):
                    pe.wait_ge(split_ready, split_no(p, c, q) + 1)
                if isinstance(c, int) and c == 0 and q % 2 == 0:
                    if p == L3:
                        pe.wait_ge(nat_used, nat_no(L2, q // 2, 1) + 1)
                    else:
                        pe.wait_ge(x_ready, q // 4 + 1 if p == L0 else PRO_GROUPS + x_no(p - 1, q // 2) + 1)
                for k in range(TQ):
                    t = TQ * q + k
                    first, end = t == 0, t == NT - 1
                    if inring:
                        hi, lo = (ringed(RINGED.index(q), part, k, 1) for part in range(2))
                    else:
                        hi, lo = (cached(c, q, part, k, 1) for part in range(2))
                    acc = accA[:, par, :]
                    both = tile(x, t, 2, 2 * D)
                    nc.tensor.matmul(acc, both, hi, start=first, stop=end and p == L0)
                    if p == L0:
                        accb = spare[0:D + 2, par, :]
                        nc.tensor.matmul(accb, tile(x, t, 0, D + 2), lo, start=first, stop=False)
                        last = nc.tensor.matmul(accb, ones16[:, :], hi, start=False, stop=end)
                    else:
                        last = nc.tensor.matmul(acc, both, lo, start=False, stop=end)
                if inring:
                    last.then_inc(ring_done, 1)

            def triangle(c, pair):
                pe.wait_ge(u_ready, NT * c + 2 * pair + 2)
                if pair >= 2 or not (isinstance(c, int) and c == 0):
                    pe.wait_ge(w_ready, 16 * c + pair - 1)
                for i in range(2):
                    t = 2 * pair + i
                    o = spare[:, 2 * (pair % 2) + i, :]
                    last = nc.tensor.matmul(o, triA[:, :], uS[:, (t % 8) * W:(t % 8 + 1) * W],
                                            start=True, stop=(t == 0))
                    if t:
                        last = nc.tensor.matmul(o, triB[:, :], uS[:, ((t - 1) % 8) * W:((t - 1) % 8 + 1) * W],
                                                start=False, stop=True)
                last.then_inc(tri_done, 1)

            def weigh(c, par, pair):
                pe.wait_ge(w_ready, 16 * c + pair + 1)
                first = 2 * HELD if isinstance(c, int) and c == 0 else 0
                for i in range(2):
                    t = 2 * pair + i
                    w = weights(c, pair)[:, i * W:(i + 1) * W].bitcast(BF16)
                    last = nc.tensor.matmul(accA[:, par, :], tile(X[L2 % 2], NT - 1 - t, 2, 2 * D), w,
                                            start=(t == first), stop=(t == NT - 1))
                last.then_inc(w_used, 1)

            def step(p, c, par, before, before2):
                for k, e in early_stages(p, c, before, before2):
                    epilogue(k, e)
                s = NC * p + c
                if not (isinstance(c, int) and c < 2 and p == L0):
                    pe.wait_ge(acc_evac, s - 1)
                    if p == L0:
                        pe.wait_ge(accb_evac, s - 1)
                if p == L3 and isinstance(c, int) and c == 0:
                    for pair in (14, 15):
                        weigh(before[1], before[2], pair)
                for b in range(NQ):
                    main(p, c, par, b, before)
                    for k, e in stages_after(p, c, par, b, before, before2):
                        epilogue(k, e)

            def finish(before, before2):
                for k, e in last_stages(before, before2):
                    epilogue(k, e)

            pe.wait_ge(const_ready, 1)
            sweep_steps(pe, step, finish)


def kernel(x, adj, L0_gnn_t, L1_gnn_W, L2_gnn_weight, L2_gnn_bias, L3_gnn_t, L3_gnn_B, L3_gnn_W1,
           L3_gnn_b1, L3_gnn_W2, L3_gnn_b2):
    import concourse.bacc as bacc
    from concourse.bass_utils import run_bass_kernel_spmd

    def host(a):
        return np.asarray(a)

    x_rows = np.ascontiguousarray(host(x).reshape(NT, P, D).transpose(1, 0, 2)).reshape(P, NT * D)
    blocks = np.ascontiguousarray(host(adj).reshape(NC, W, NQ, TQ, P).transpose(0, 2, 4, 3, 1))
    blocks = blocks.reshape(NC * NQ * P, BLK)

    wts = np.zeros((P, NCOLS), np.float32)

    def put(name, a):
        lo, hi = COLS[name]
        wts[0:a.shape[0], lo:hi] = a

    for k in range(2):
        for h in range(2):
            lo, hi = COLS[f"wagg{k}"]
            wts[h * D:(h + 1) * D, lo:hi] = host(L1_gnn_W)[k, 0:D]
            lo, hi = COLS[f"wx{k}"]
            wts[h * D:(h + 1) * D, lo:hi] = host(L1_gnn_W)[k, D:2 * D]
    put("l2w", host(L2_gnn_weight))
    put("bT", host(L3_gnn_B).T)
    put("w1", host(L3_gnn_W1)[0:D])
    put("w2", host(L3_gnn_W2).reshape(2, P, D).transpose(1, 0, 2).reshape(P, 2 * D))
    put("w1t", host(L3_gnn_W1)[D].reshape(2, P).T)
    put("b1", host(L3_gnn_b1).reshape(2, P).T)
    put("t", np.broadcast_to(host(L3_gnn_t).reshape(1, 1), (P, 1)))
    put("bias", np.broadcast_to(host(L2_gnn_bias).reshape(1, D), (P, D)))
    put("b2", np.broadcast_to(host(L3_gnn_b2).reshape(1, D), (P, D)))
    put("ident", np.eye(P, dtype=np.float32))
    eye = np.eye(D, dtype=np.float32)
    put("joinA", np.concatenate([np.concatenate([eye, eye], 0), np.zeros((P, 1), np.float32)], 1))
    join_b = np.zeros((P, D + 1), np.float32)
    join_b[2:2 + D, 0:D] = eye
    join_b[0, D] = 1.0
    put("joinB", join_b)
    i, j = np.arange(P)[:, None], np.arange(P)[None, :]
    tri_a = np.where(i > j, -BIT, np.where(i == j, NEIGH * BIT, 0.0)).astype(np.float32)
    tri_b = np.float32(-BIT) - tri_a
    tri = np.concatenate([tri_a, tri_b], 1)

    nc = bacc.Bacc("TRN2", target_bir_lowering=False, num_devices=1)
    arrays = {"x_rows": x_rows, "adj_blocks": blocks, "weights": wts, "triangles": tri}
    args = [nc.dram_tensor(n, a.shape, mybir.dt.from_np(a.dtype), kind="ExternalInput").ap()
            for n, a in arrays.items()]
    out = nc.dram_tensor("out_rows", (P, NT * D), F32, kind="ExternalOutput").ap()
    gnn_kernel(nc, *args, out)
    r = run_bass_kernel_spmd(nc, [arrays], core_ids=[0])
    got = r.results[0]["out_rows"]
    return np.ascontiguousarray(got.reshape(P, NT, D).transpose(1, 0, 2)).reshape(N, D)
```
